# Optimizing a Trainium2 kernel written in Bass

```python
import numpy as np
import jax
import jax.numpy as jnp

def _softmax(x, axis=-1):
    return jax.nn.softmax(x, axis=axis)

def _gelu(x):
    return jax.nn.gelu(x, approximate=True)

def _silu(x):
    return jax.nn.silu(x)

def _sigmoid(x):
    return jax.nn.sigmoid(x)

def _layernorm(x, axis=-1, eps=1e-05):
    m = jnp.mean(x, axis=axis, keepdims=True)
    v = jnp.var(x, axis=axis, keepdims=True)
    return (x - m) / jnp.sqrt(v + eps)

def _scatter_add(tgt, idx, src, axis=0):
    return tgt.at[idx].add(src)

def _segment_sum(src, seg, n):
    return jax.ops.segment_sum(src, seg, n)
kernel_name = 'mk_gnn_preln_d2_gnn_r8_2914dc'

def setup_inputs(seed: int=0):
    np.random.seed(seed)
    _w = jnp.asarray

    def _rec_inputs():
        import jax
        import jax.numpy as jnp
        _gk = jax.random.key(seed)
        x = -0.0005121 + 1.001 * jax.random.normal(jax.random.fold_in(_gk, 1), (6250, 64), jnp.float32)
        _s = jax.random.randint(jax.random.fold_in(_gk, 2), (100000,), 0, 6250, jnp.int32)
        _d = jax.random.randint(jax.random.fold_in(_gk, 3), (100000,), 0, 6250, jnp.int32)
        _loop = jnp.arange(6250, dtype=jnp.int32)
        src = jnp.concatenate([_s, _d, _loop])
        dst = jnp.concatenate([_d, _s, _loop])
        _o = jnp.argsort(dst, stable=True)
        src = src[_o]
        dst = dst[_o]
        edge_attr_16 = 0.000254156 + 0.999948 * jax.random.normal(jax.random.fold_in(_gk, 11), (206250, 16), jnp.float32)
        edge_attr_32 = -5.3897e-05 + 0.999841 * jax.random.normal(jax.random.fold_in(_gk, 12), (206250, 32), jnp.float32)
        return (x, src, dst, edge_attr_16, edge_attr_32)
    x, src, dst, edge_attr_16, edge_attr_32 = _rec_inputs()

    def _L0_gnn_setup():
        import jax, jax.numpy as jnp
        import numpy as np
        N, E = (6250, 100000)
        IN_DIM, EDGE_DIM, OUT_DIM = (64, 16, 64)
        key = jax.random.key(seed)
        k1, k2, k3, k4, k5, k6, k7 = jax.random.split(key, 7)
        x = jax.random.normal(k1, (N, IN_DIM), dtype=jnp.float32)
        edge_index = jax.random.randint(k2, (2, E), 0, N, dtype=jnp.int64)
        edge_attr = jax.random.normal(k3, (E, EDGE_DIM), dtype=jnp.float32)
        s1 = 1.0 / np.sqrt(IN_DIM + EDGE_DIM)
        W1 = jax.random.uniform(k4, (IN_DIM + EDGE_DIM, OUT_DIM), jnp.float32, -s1, s1)
        b1 = jax.random.uniform(k5, (OUT_DIM,), jnp.float32, -s1, s1)
        s2 = 1.0 / np.sqrt(IN_DIM)
        Wres = jax.random.uniform(k6, (IN_DIM, OUT_DIM), jnp.float32, -s2, s2)
        bres = jax.random.uniform(k7, (OUT_DIM,), jnp.float32, -s2, s2)
        return {'x': x, 'edge_index': edge_index, 'edge_attr': edge_attr, 'W1': W1, 'b1': b1, 'Wres': Wres, 'bres': bres}
    _L0_gnn_all = _L0_gnn_setup()
    _L0_gnn_in = {k: v for k, v in _L0_gnn_all.items() if k in ('W1', 'b1', 'Wres', 'bres')}
    del _L0_gnn_all

    def _L1_gnn_setup():
        import jax, jax.numpy as jnp
        import numpy as np
        N = 6250
        E = 100000
        DIN = 64
        DE = 32
        HID = 32
        DOUT = 64

        def _lin_init(key, fan_in, fan_out):
            return jax.random.normal(key, (fan_in, fan_out), dtype=jnp.float32) / np.sqrt(fan_in)

        def _transformer_conv(x, src, dst, eattr, Wq, bq, Wk, bk, Wv, bv, We, Ws, bs, H, C, concat):
            n = x.shape[0]
            q = (x @ Wq + bq).reshape(n, H, C)
            k = (x @ Wk + bk).reshape(n, H, C)
            v = (x @ Wv + bv).reshape(n, H, C)
            e = (eattr @ We).reshape(-1, H, C)
            kj = k[src] + e
            alpha = jnp.sum(q[dst] * kj, axis=-1) / jnp.sqrt(jnp.float32(C))
            m = jax.ops.segment_max(alpha, dst, num_segments=n)
            a = jnp.exp(alpha - m[dst])
            s = jax.ops.segment_sum(a, dst, num_segments=n)
            a = a / (s[dst] + 1e-16)
            vj = v[src] + e
            out = jax.ops.segment_sum(a[..., None] * vj, dst, num_segments=n)
            out = out.reshape(n, H * C) if concat else jnp.mean(out, axis=1)
            return out + x @ Ws + bs
        key = jax.random.key(seed)
        ks = list(jax.random.split(key, 64))
        inp = {}
        inp['x'] = jax.random.normal(ks[0], (N, DIN), dtype=jnp.float32)
        inp['edge_attr'] = jax.random.normal(ks[1], (E, DE), dtype=jnp.float32)
        inp['edge_index'] = jax.random.randint(ks[2], (2, E), 0, N, dtype=jnp.int32)
        dims = [(DIN, 2, HID, 2 * HID), (2 * HID, 2, HID, 2 * HID), (2 * HID, 1, DOUT, DOUT)]
        ki = 3
        for l, (din, H, C, dskip) in enumerate(dims):
            HC = H * C
            inp[f'Wq{l}'] = _lin_init(ks[ki], din, HC)
            ki += 1
            inp[f'bq{l}'] = jnp.zeros((HC,), jnp.float32)
            inp[f'Wk{l}'] = _lin_init(ks[ki], din, HC)
            ki += 1
            inp[f'bk{l}'] = jnp.zeros((HC,), jnp.float32)
            inp[f'Wv{l}'] = _lin_init(ks[ki], din, HC)
            ki += 1
            inp[f'bv{l}'] = jnp.zeros((HC,), jnp.float32)
            inp[f'We{l}'] = _lin_init(ks[ki], DE, HC)
            ki += 1
            inp[f'Ws{l}'] = _lin_init(ks[ki], din, dskip)
            ki += 1
            inp[f'bs{l}'] = jnp.zeros((dskip,), jnp.float32)
        inp['prelu_a'] = jnp.asarray(0.25, dtype=jnp.float32)
        return inp
    _L1_gnn_all = _L1_gnn_setup()
    _L1_gnn_in = {k: v for k, v in _L1_gnn_all.items() if k in ('Wq0', 'bq0', 'Wk0', 'bk0', 'Wv0', 'bv0', 'We0', 'Ws0', 'bs0', 'Wq1', 'bq1', 'Wk1', 'bk1', 'Wv1', 'bv1', 'We1', 'Ws1', 'bs1', 'Wq2', 'bq2', 'Wk2', 'bk2', 'Wv2', 'bv2', 'We2', 'Ws2', 'bs2', 'prelu_a')}
    del _L1_gnn_all
    return {'x': x, 'src': src, 'dst': dst, 'edge_attr_16': edge_attr_16, 'edge_attr_32': edge_attr_32, 'L0_gnn_W1': _L0_gnn_in['W1'], 'L0_gnn_b1': _L0_gnn_in['b1'], 'L0_gnn_Wres': _L0_gnn_in['Wres'], 'L0_gnn_bres': _L0_gnn_in['bres'], 'L1_gnn_Wq0': _L1_gnn_in['Wq0'], 'L1_gnn_bq0': _L1_gnn_in['bq0'], 'L1_gnn_Wk0': _L1_gnn_in['Wk0'], 'L1_gnn_bk0': _L1_gnn_in['bk0'], 'L1_gnn_Wv0': _L1_gnn_in['Wv0'], 'L1_gnn_bv0': _L1_gnn_in['bv0'], 'L1_gnn_We0': _L1_gnn_in['We0'], 'L1_gnn_Ws0': _L1_gnn_in['Ws0'], 'L1_gnn_bs0': _L1_gnn_in['bs0'], 'L1_gnn_Wq1': _L1_gnn_in['Wq1'], 'L1_gnn_bq1': _L1_gnn_in['bq1'], 'L1_gnn_Wk1': _L1_gnn_in['Wk1'], 'L1_gnn_bk1': _L1_gnn_in['bk1'], 'L1_gnn_Wv1': _L1_gnn_in['Wv1'], 'L1_gnn_bv1': _L1_gnn_in['bv1'], 'L1_gnn_We1': _L1_gnn_in['We1'], 'L1_gnn_Ws1': _L1_gnn_in['Ws1'], 'L1_gnn_bs1': _L1_gnn_in['bs1'], 'L1_gnn_Wq2': _L1_gnn_in['Wq2'], 'L1_gnn_bq2': _L1_gnn_in['bq2'], 'L1_gnn_Wk2': _L1_gnn_in['Wk2'], 'L1_gnn_bk2': _L1_gnn_in['bk2'], 'L1_gnn_Wv2': _L1_gnn_in['Wv2'], 'L1_gnn_bv2': _L1_gnn_in['bv2'], 'L1_gnn_We2': _L1_gnn_in['We2'], 'L1_gnn_Ws2': _L1_gnn_in['Ws2'], 'L1_gnn_bs2': _L1_gnn_in['bs2'], 'L1_gnn_prelu_a': _L1_gnn_in['prelu_a']}

def reference(x, src, dst, edge_attr_16, edge_attr_32, L0_gnn_W1, L0_gnn_b1, L0_gnn_Wres, L0_gnn_bres, L1_gnn_Wq0, L1_gnn_bq0, L1_gnn_Wk0, L1_gnn_bk0, L1_gnn_Wv0, L1_gnn_bv0, L1_gnn_We0, L1_gnn_Ws0, L1_gnn_bs0, L1_gnn_Wq1, L1_gnn_bq1, L1_gnn_Wk1, L1_gnn_bk1, L1_gnn_Wv1, L1_gnn_bv1, L1_gnn_We1, L1_gnn_Ws1, L1_gnn_bs1, L1_gnn_Wq2, L1_gnn_bq2, L1_gnn_Wk2, L1_gnn_bk2, L1_gnn_Wv2, L1_gnn_bv2, L1_gnn_We2, L1_gnn_Ws2, L1_gnn_bs2, L1_gnn_prelu_a):
    import jax
    import jax.numpy as jnp

    def _L0_gnn_ref(x, edge_index, edge_attr, W1, b1, Wres, bres):
        import jax, jax.numpy as jnp
        import numpy as np
        N, E = (6250, 100000)
        IN_DIM, EDGE_DIM, OUT_DIM = (64, 16, 64)
        dst = edge_index[1]
        x_i = x[dst]
        msg_in = jnp.concatenate([x_i, edge_attr], axis=-1)
        msg = jax.nn.relu(msg_in @ W1 + b1)
        summed = jax.ops.segment_sum(msg, dst, num_segments=N)
        count = jax.ops.segment_sum(jnp.ones((msg.shape[0],), msg.dtype), dst, num_segments=N)
        aggr = summed / jnp.maximum(count, 1.0)[:, None]
        res = x @ Wres + bres
        return jax.nn.relu(aggr + res)

    def _L1_gnn_ref(x, edge_attr, edge_index, Wq0, bq0, Wk0, bk0, Wv0, bv0, We0, Ws0, bs0, Wq1, bq1, Wk1, bk1, Wv1, bv1, We1, Ws1, bs1, Wq2, bq2, Wk2, bk2, Wv2, bv2, We2, Ws2, bs2, prelu_a):
        import jax, jax.numpy as jnp
        import numpy as np
        N = 6250
        E = 100000
        DIN = 64
        DE = 32
        HID = 32
        DOUT = 64

        def _lin_init(key, fan_in, fan_out):
            return jax.random.normal(key, (fan_in, fan_out), dtype=jnp.float32) / np.sqrt(fan_in)

        def _transformer_conv(x, src, dst, eattr, Wq, bq, Wk, bk, Wv, bv, We, Ws, bs, H, C, concat):
            n = x.shape[0]
            q = (x @ Wq + bq).reshape(n, H, C)
            k = (x @ Wk + bk).reshape(n, H, C)
            v = (x @ Wv + bv).reshape(n, H, C)
            e = (eattr @ We).reshape(-1, H, C)
            kj = k[src] + e
            alpha = jnp.sum(q[dst] * kj, axis=-1) / jnp.sqrt(jnp.float32(C))
            m = jax.ops.segment_max(alpha, dst, num_segments=n)
            a = jnp.exp(alpha - m[dst])
            s = jax.ops.segment_sum(a, dst, num_segments=n)
            a = a / (s[dst] + 1e-16)
            vj = v[src] + e
            out = jax.ops.segment_sum(a[..., None] * vj, dst, num_segments=n)
            out = out.reshape(n, H * C) if concat else jnp.mean(out, axis=1)
            return out + x @ Ws + bs
        src, dst = (edge_index[0], edge_index[1])
        h = _transformer_conv(x, src, dst, edge_attr, Wq0, bq0, Wk0, bk0, Wv0, bv0, We0, Ws0, bs0, 2, HID, True)
        h = jnp.where(h >= 0, h, prelu_a * h)
        h = _transformer_conv(h, src, dst, edge_attr, Wq1, bq1, Wk1, bk1, Wv1, bv1, We1, Ws1, bs1, 2, HID, True)
        h = jnp.where(h >= 0, h, prelu_a * h)
        h = _transformer_conv(h, src, dst, edge_attr, Wq2, bq2, Wk2, bk2, Wv2, bv2, We2, Ws2, bs2, 1, DOUT, False)
        return h
    edge_index = jnp.stack([src, dst])
    h = jnp.maximum(_layernorm(x, axis=-1), 0.0)
    x = x + _L0_gnn_ref(h, edge_index, edge_attr_16, L0_gnn_W1, L0_gnn_b1, L0_gnn_Wres, L0_gnn_bres)
    h = jnp.maximum(_layernorm(x, axis=-1), 0.0)
    x = x + _L1_gnn_ref(h, edge_attr_32, edge_index, L1_gnn_Wq0, L1_gnn_bq0, L1_gnn_Wk0, L1_gnn_bk0, L1_gnn_Wv0, L1_gnn_bv0, L1_gnn_We0, L1_gnn_Ws0, L1_gnn_bs0, L1_gnn_Wq1, L1_gnn_bq1, L1_gnn_Wk1, L1_gnn_bk1, L1_gnn_Wv1, L1_gnn_bv1, L1_gnn_We1, L1_gnn_Ws1, L1_gnn_bs1, L1_gnn_Wq2, L1_gnn_bq2, L1_gnn_Wk2, L1_gnn_bk2, L1_gnn_Wv2, L1_gnn_bv2, L1_gnn_We2, L1_gnn_Ws2, L1_gnn_bs2, L1_gnn_prelu_a)
    return x

_drawn_inputs = setup_inputs


def setup_inputs(seed=0):
    import zlib

    import numpy as np

    out = dict(_drawn_inputs(seed))
    spreads = {'L1_gnn_bq0': (0.0, 0.517),
     'L1_gnn_bk0': (0.0, 0.8),
     'L1_gnn_bv0': (0.0, 0.1),
     'L1_gnn_bs0': (0.0, 0.1),
     'L1_gnn_bq1': (0.0, 0.3),
     'L1_gnn_bk1': (0.0, 0.8),
     'L1_gnn_bv1': (0.0, 0.1),
     'L1_gnn_bs1': (0.0, 0.1),
     'L1_gnn_bq2': (0.0, 0.339),
     'L1_gnn_bk2': (0.0, 0.8),
     'L1_gnn_bv2': (0.0, 0.1),
     'L1_gnn_bs2': (0.0, 0.1)}
    factors = {'edge_attr_16': 2.794}
    for name, (base, spread) in spreads.items():
        noise = np.random.default_rng([zlib.crc32(name.encode()), seed]).standard_normal(out[name].shape)
        drawn = base * np.exp(spread * noise) if base else spread * noise
        out[name] = jnp.asarray(drawn.astype(out[name].dtype))
    for name, factor in factors.items():
        out[name] = (out[name] * factor).astype(out[name].dtype)
    return out
```

```python
import numpy as np
from contextlib import ExitStack

import concourse.bass as bass
from concourse import mybir

F32 = mybir.dt.float32
I32 = mybir.dt.int32
ALU = mybir.AluOpType
ACT = mybir.ActivationFunctionType
AX = mybir.AxisListType
BIG = 1.0e30
EPS = 1e-5

T = 8
BE = 128 * T
W = 64


class Sizes:
    def __init__(self, n, e):
        self.n = n
        self.e = e
        self.blocks = -(-e // BE)
        self.blocks += self.blocks % 2
        self.tiles = -(-(n + 1 + W) // 128)
        self.nc = self.tiles * 128
        self.idle = n + 1
        self.smax = W + self.blocks + -(-(n + 1) // W) + 3
        assert self.idle + W <= self.nc and self.smax <= 512


class At:

    def __init__(self, i, c):
        self.i, self.c = i, c

    def __add__(self, d):
        return At(self.i, self.c + d)

    def __sub__(self, d):
        return At(self.i, self.c - d)

    @property
    def slot(self):
        return self.c % 3

    def times(self, k, add):
        return self.i * k + (self.c // 3 * k + add)

    def value(self):
        return self.i * 3 + self.c


def gnn_program(nc, z, a):
    ctx = ExitStack()
    with ctx:
        build(nc, z, a, ctx)


def build(nc, z, a, ctx):
    B, NCOL, NT, SM = z.blocks, z.nc, z.tiles, z.smax
    N = z.n

    def sb(name, shape, dt=F32):
        return ctx.enter_context(nc.sbuf_tensor(name, shape, dt))

    def pb(name, shape, dt=F32):
        return ctx.enter_context(nc.psum_tensor(name, shape, dt))

    def sem(name):
        return ctx.enter_context(nc.semaphore(name))

    XR = sb("XR", [128, NT, 64])
    WK = sb("WK", [128, NT, 64])
    hT = sb("hT", [65, NCOL])
    acc = sb("acc", [128, NCOL])
    st = sb("st", [128, 4, NT])
    w1 = sb("w1", [65, 64])
    wr = sb("wr", [65, 64])
    bd16 = sb("bd16", [128, T * 64])
    wkvq = sb("wkvq", [65, 3, 192])
    bd32 = sb("bd32", [128, 3, 256])
    wskip = sb("wskip", [65, 3, 64])
    pra = sb("pra", [64, 1])
    ident = sb("ident", [128, 128])
    cmat = sb("cmat", [128, W])
    e0 = sb("e0", [64, 1])
    ioi = sb("ioi", [128, SM], I32)
    iof = sb("iof", [128, SM])
    bf = sb("bf", [128, SM])
    tbl = sb("tbl", [128, 2, SM], I32)
    ntr = sb("ntr", [128, 1], I32)
    fl = sb("fl", [1, 2, B], I32)
    flf = sb("flf", [1, 2, B])
    wi = sb("wi", [1, 2, B], I32)
    pe_ = sb("pe_", [1, 4, B + 1])
    pcol = sb("pcol", [128, 2, 2])
    cmp_ = sb("cmp_", [128, 2, SM])
    dlh = sb("dlh", [128, 2, 128])
    ones = sb("ones", [128, 128])
    n3 = sb("n3", [1, 2, SM])
    fbuf = sb("fbuf", [64, 2, 512])
    stg = sb("stg", [128, 2, 4, 192])

    G = [sb(f"G{u}", [128, T, 128]) for u in range(3)]
    sdn = [sb(f"sdn{u}", [128, 3 * T], I32) for u in range(3)]
    ea = [sb(f"ea{u}", [128, 256]) for u in range(3)]
    dr = [sb(f"dr{u}", [16, 128], I32) for u in range(3)]
    qw = [sb(f"qw{u}", [W, 64]) for u in range(3)]
    O = [sb(f"O{u}", [128, T, W]) for u in range(3)]
    OTs = [sb(f"OTs{u}", [W, T, 128]) for u in range(3)]
    kj = sb("kj", [128, T, 64])
    vj = [sb(f"vj{u}", [128, T, 64]) for u in range(3)]
    vals = [sb(f"vals{u}", [128, T, 128]) for u in range(3)]
    al = [sb(f"al{u}", [128, 2 * T]) for u in range(3)]
    tb = [sb(f"tb{u}", [16, 128]) for u in range(3)]
    flg = sb("flg", [16, 128])
    Fs = sb("Fs", [16, 128])
    fw = [sb(f"fw{u}", [128, T, 4]) for u in range(3)]
    cont = [sb(f"cont{u}", [128, 1]) for u in range(3)]
    cr = sb("cr", [128, 4])
    pbm = sb("pbm", [W, T + 1])
    X = sb("X", [W, 2, T + 1])
    Mm = sb("Mm", [W, 4])
    df = sb("df", [W, 2])
    fb = sb("fb", [W, 128])
    dd = sb("dd", [128, T, 2])

    pE = [pb(f"pE{u}", [128, T * 64]) for u in range(3)]
    pOT = pb("pOT", [W, T * 128])
    pQ = pb("pQ", [128, 512])
    pY = pOT[:, 0:512]
    pS = pb("pS", [128, 512])
    pG = pb("pG", [128, 512])
    pAT = pS[0:16, 0:128]
    pFb = pS[:, 128:144]
    pMn = pS[0:W, 160:160 + 4 * (T + 1)]
    pMe = pS[:, 200:200 + 4 * T]
    pFac = pG[:, 64:65]

    def dram(name, shape):
        return nc.dram_tensor(name, shape, F32, kind="Internal").ap()

    PT = dram("PT", [NCOL, 64])
    KV = [dram(f"KV{l}", [NCOL, 128]) for l in range(3)]
    QT = [dram(f"QT{l}", [NCOL, 64]) for l in range(3)]

    queue = {k: [] for k in "VAPGS"}
    done = {k: sem(f"done_{k}") for k in "VAPG"}
    count = dict.fromkeys("VAPG", 0)

    def op(k, f, *waits):
        count[k] += 1

        def run(e):
            for s, v in waits:
                e.wait_ge(s, v)
            f(e).then_inc(done[k], 1)
        queue[k].append(run)
        return done[k], count[k]

    def dma(k, s, n, f, *waits):
        def run(e):
            for q, v in waits:
                e.wait_ge(q, v)
            f(e).then_inc(s, 16)
        queue[k].append(run)
        return s, n

    def last(k):
        return done[k], count[k]

    s_w = sem("s_w")
    nw = [0]

    def load(out, src, k="S"):
        nw[0] += 16
        dma(k, s_w, nw[0], lambda e, out=out, src=src: e.dma_start(out, src))

    def row(v, m):
        return v.rearrange("(a m) -> a m", a=1) if m else v

    s_x = sem("s_x")
    s_fl = sem("s_fl")
    x_t = dma("S", s_x, 16, lambda e: e.dma_start(XR[:, :, :], a["x"].rearrange("(t p) c -> p t c", p=128)))
    dma("A", s_fl, 16, lambda e: e.dma_start(fl[:, 0, :], a["dst_first"]))
    fl_t = dma("A", s_fl, 32, lambda e: e.dma_start(fl[:, 1, :], a["dst_last"]))

    zb = op("V", lambda e: e.memset(bd16[:, :], 0.0))
    zb2 = op("V", lambda e: e.memset(bd32[:, :, :], 0.0))
    queue["S"].append(lambda e: e.wait_ge(*zb2))
    load(w1[0:64, :], a["W1"][0:64, :])
    load(w1[64:65, :], row(a["b1"], 1))
    load(wr[0:64, :], a["Wres"])
    load(wr[64:65, :], row(a["bres"], 1))
    for j in range(T):
        load(bd16[16 * j:16 * j + 16, 64 * j:64 * j + 64], a["W1"][64:80, :])
    for l in range(3):
        for m, c in enumerate("kvq"):
            load(wkvq[0:64, l, 64 * m:64 * m + 64], a[f"W{c}{l}"])
            load(wkvq[64:65, l, 64 * m:64 * m + 64], row(a[f"b{c}{l}"], 1))
        for j in range(4):
            load(bd32[32 * j:32 * j + 32, l, 64 * j:64 * j + 64], a[f"We{l}"])
        load(wskip[0:64, l, :], a[f"Ws{l}"])
        load(wskip[64:65, l, :], row(a[f"bs{l}"], 1))
    load(pra[:, :], a["prelu"].rearrange("(a m) -> a m", a=1).to_broadcast([64, 1]))
    w_t = (s_w, nw[0])

    op("G", lambda e: e.memset(ident[:, :], 0.0))
    op("G", lambda e: e.memset(cmat[:, :], 0.0))
    op("G", lambda e: e.memset(e0[:, :], 0.0))
    g0 = op("G", lambda e: e.memset(ones[:, :], 1.0))
    op("G", lambda e: e.affine_select(out=ident[:, :], in_=ident[:, :], compare_op=ALU.not_equal, fill=1.0,
                                      base=0, pattern=[[-1, 128]], channel_multiplier=1), g0)
    op("G", lambda e: e.affine_select(out=cmat[:, :], in_=cmat[:, :], compare_op=ALU.not_equal, fill=1.0,
                                      base=-127, pattern=[[W, W]], channel_multiplier=1))
    op("G", lambda e: e.affine_select(out=e0[:, :], in_=e0[:, :], compare_op=ALU.not_equal, fill=1.0,
                                      base=0, pattern=[[1, 1]], channel_multiplier=1))
    op("G", lambda e: e.iota(ioi[:, :], pattern=[[1, SM]], base=0, channel_multiplier=0))
    g_t = last("G")
    io_t = op("V", lambda e: e.tensor_copy(iof[:, :], ioi[:, :]), g_t)

    op("V", lambda e: e.tensor_copy(flf[:, :, :], fl[:, :, :]), fl_t)
    v = op("V", lambda e: e.tensor_tensor(wi[:, 0, :], fl[:, 1, :], fl[:, 0, :], ALU.subtract))
    v = op("V", lambda e: e.tensor_scalar(wi[:, 1, :], wi[:, 0, :], 6, None, ALU.arith_shift_right), v)
    v = op("V", lambda e: e.memset(pe_[:, :, :], 0.0), v)
    v = op("V", lambda e: e.memset(pe_[:, 3, :], 1.0), v)
    v = op("V", lambda e: e.tensor_copy(pe_[:, 0, 0:B], wi[:, 1, :]), v)
    v = op("V", lambda e: e.tensor_scalar(pe_[:, 0, 0:B], pe_[:, 0, 0:B], 1.0, None, ALU.add), v)
    v = op("V", lambda e: e.tensor_tensor_scan(pe_[:, 1, 1:B + 1], pe_[:, 3, 0:B], pe_[:, 0, 0:B], 0.0,
                                               ALU.mult, ALU.add), v)
    v = op("V", lambda e: e.scalar_tensor_tensor(pe_[:, 2, 0:B], pe_[:, 1, 0:B], -float(W), flf[:, 0, :],
                                                 ALU.mult, ALU.add), v)
    v = op("V", lambda e: e.tensor_tensor(pe_[:, 0, 0:B - 1], pe_[:, 2, 1:B], pe_[:, 2, 0:B - 1], ALU.subtract), v)
    v = op("V", lambda e: e.memset(pe_[:, 0, B - 1:B], 0.0), v)
    HB = B // 2
    for k in range(2):
        op("P", lambda e, k=k: e.matmul(pQ[0:HB, k:k + 1], pe_[:, 1, 1 + k:B + 1:2], ones[0:1, 0:1],
                                        start=True, stop=True), v, g_t)
        op("P", lambda e, k=k: e.matmul(pQ[0:HB, 2 + k:3 + k], pe_[:, 0, k:B:2], ones[0:1, 0:1],
                                        start=True, stop=True))
    p = op("P", lambda e: e.matmul(pQ[:, 4:5], ones[0:1, :], flf[:, 0, 0:1], start=True, stop=True))
    v = op("V", lambda e: e.tensor_copy(pcol[0:HB, :, :], pQ[0:HB, 0:4].rearrange("p (a b) -> p a b", a=2)), p)
    f0 = sb("f0", [128, 1])
    op("V", lambda e: e.tensor_copy(f0[:, :], pQ[:, 4:5]))
    for k in range(2):
        op("V", lambda e, k=k: e.tensor_scalar(cmp_[0:HB, k, :], iof[0:HB, :], pcol[0:HB, 0, k:k + 1], None,
                                               ALU.is_ge), v)
        v2 = op("V", lambda e, k=k: e.tensor_scalar(dlh[0:HB, k, :], ones[0:HB, :], pcol[0:HB, 1, k:k + 1], None,
                                                    ALU.mult))
    for k in range(2):
        op("P", lambda e, k=k: e.matmul(pS[:, 0:SM], ones[0:HB, :], cmp_[0:HB, k, :],
                                        start=k == 0, stop=k == 1), v2)
    for k in range(2):
        p = op("P", lambda e, k=k: e.matmul(pG[:, 0:SM], dlh[0:HB, k, :], cmp_[0:HB, k, :],
                                            start=k == 0, stop=k == 1))
    idle = float(z.idle)
    v = op("V", lambda e: e.scalar_tensor_tensor(bf[:, :], iof[:, :], float(W), pG[:, 0:SM], ALU.mult, ALU.add), p)
    v = op("V", lambda e: e.tensor_scalar(bf[:, :], bf[:, :], f0[:, 0:1], idle, ALU.add, ALU.min), v)
    v3 = op("V", lambda e: e.tensor_scalar(cmp_[:, 0, :], pS[:, 0:SM], float(B), idle, ALU.is_ge, ALU.mult), v)
    v = op("V", lambda e: e.tensor_tensor(bf[:, :], bf[:, :], cmp_[:, 0, :], ALU.max), v3)
    op("V", lambda e: e.tensor_copy(tbl[:, 1, :], bf[:, :]), v)
    op("V", lambda e: e.tensor_scalar(tbl[:, 0, :], pS[:, 0:SM], float(B - 1), None, ALU.min))
    v = op("V", lambda e: e.tensor_scalar(n3[:, 0, :], iof[0:1, :], 3.0, 2.0, ALU.mult, ALU.add))
    v = op("V", lambda e: e.tensor_scalar(n3[:, 0, :], n3[:, 0, :], pe_[:, 1, B:B + 1], None, ALU.is_le), v)
    v = op("V", lambda e: e.tensor_reduce(n3[:, 1, 0:1], n3[:, 0, :], AX.X, ALU.add), v)
    t_t = op("V", lambda e: e.tensor_copy(ntr[0:1, :], n3[:, 1, 0:1]), v)
    op("V", lambda e: e.memset(hT[64:65, :], 1.0))
    op("V", lambda e: e.memset(pMe, 0.0))
    op("V", lambda e: e.memset(flg[:, :], 0.0))
    op("V", lambda e: e.memset(acc[:, :], 0.0))
    for u in range(3):
        op("V", lambda e, u=u: e.memset(vals[u][:, :, 64:128], 1.0))

    def norm_rows(xt):
        bank = [pQ, pY]
        v = op("V", lambda e: e.tensor_reduce(st[:, 0, :], XR[:, :, :], AX.X, ALU.add), xt)
        v = op("V", lambda e: e.tensor_scalar(st[:, 0, :], st[:, 0, :], 1.0 / 64, None, ALU.mult), v)
        v = op("V", lambda e: e.tensor_tensor(WK[:, :, :], XR[:, :, :], st[:, 0, :].unsqueeze(2).to_broadcast(
            [128, NT, 64]), ALU.subtract), v)
        sq = acc[:, 0:NT * 64].rearrange("p (t c) -> p t c", c=64)
        v = op("V", lambda e: e.tensor_tensor(sq, WK[:, :, :], WK[:, :, :], ALU.mult), v)
        v = op("V", lambda e: e.tensor_reduce(st[:, 1, :], sq, AX.X, ALU.add), v)
        v = op("V", lambda e: e.tensor_scalar(st[:, 1, :], st[:, 1, :], 1.0 / 64, EPS, ALU.mult, ALU.add), v)
        s = op("A", lambda e: e.activation(st[:, 2, :], st[:, 1, :], ACT.Sqrt), v)
        v = op("V", lambda e: e.reciprocal(st[:, 3, :], st[:, 2, :]), s)
        v = op("V", lambda e: e.tensor_tensor(WK[:, :, :], WK[:, :, :], st[:, 3, :].unsqueeze(2).to_broadcast(
            [128, NT, 64]), ALU.mult), v)
        op("V", lambda e: e.memset(acc[:, 0:NT * 64], 0.0))
        evs = []
        for c in range(-(-NT // 4)):
            m = min(4, NT - 4 * c)
            for j in range(m):
                w = [v, g_t] if c < 2 else [evs[c - 2]]
                pt = op("P", lambda e, c=c, j=j: e.transpose(bank[c % 2][0:64, 128 * j:128 * j + 128],
                                                             WK[:, 4 * c + j, :], ident[:, :]), *w)
            evs.append(op("A", lambda e, c=c, m=m: e.activation(
                hT[0:64, 512 * c:512 * c + 128 * m], bank[c % 2][0:64, 0:128 * m], ACT.Relu), pt))
        return evs

    s_t = [sem(f"s_t{l}") for l in range(2)]
    nt = [0, 0]

    def tables(evs, lhs_n, weights, outs):
        bank = [pE[0], pE[1]]
        free = []
        for c in range(-(-NT // 2)):
            m = min(2, NT - 2 * c)
            g = (c // 2) % 2
            for j in range(m):
                w = [evs[c // 2]] + ([free[c - 2]] if c >= 2 else [w_t])
                pt = op("P", lambda e, c=c, j=j: e.matmul(
                    bank[c % 2][:, lhs_n * j:lhs_n * j + lhs_n], hT[:, 256 * c + 128 * j:256 * c + 128 * j + 128],
                    weights, start=True, stop=True), *w)
            w = [pt] + ([(s_t[g], nt[g])] if c % 2 == 0 and nt[g] else [])
            ev = op("A", lambda e, c=c, m=m, g=g: e.activation(
                stg[:, g, 2 * (c % 2):2 * (c % 2) + m, 0:lhs_n],
                bank[c % 2][:, 0:lhs_n * m].rearrange("p (t c) -> p t c", t=m), ACT.Copy), *w)
            free.append(ev)
            if c % 2 == 1 or 2 * c + m >= NT:
                t0, tn = 4 * (c // 2), min(4, NT - 4 * (c // 2))
                for tab, c0, cn in outs:
                    nt[g] += 16
                    dma("S", s_t[g], nt[g], lambda e, tab=tab, t0=t0, tn=tn, g=g, c0=c0, cn=cn: e.dma_start(
                        tab[128 * t0:128 * (t0 + tn), :].rearrange("(t p) c -> p t c", p=128),
                        stg[:, g, 0:tn, c0:c0 + cn]), ev)
        return [(s_t[0], nt[0]), (s_t[1], nt[1])]

    def fold(kind, l, vt):
        bank = [pQ, pY]
        evs = []
        lhs = wr[:, :] if kind == "mean" else wskip[:, l, :]
        for c in range(-(-NCOL // 512)):
            n = min(512, NCOL - 512 * c)
            sl = slice(512 * c, 512 * c + n)
            wc = slice(0, n)
            buf = fbuf[:, 0, 0:n]
            buf2 = fbuf[:, 1, 0:n]
            w = [w_t, vt] if c < 2 else [evs[c - 2]]
            pt = op("P", lambda e, c=c, sl=sl, n=n: e.matmul(bank[c % 2][0:64, 0:n], lhs, hT[:, sl],
                                                             start=True, stop=True), *w)
            v = last("V")
            if kind == "mean":
                v = op("V", lambda e, sl=sl, buf=buf: e.tensor_scalar(buf, acc[64:128, sl], 1.0, None, ALU.max), vt, v)
            else:
                v = op("V", lambda e, sl=sl, buf=buf: e.tensor_scalar(buf, acc[64:128, sl], 1e-16, None, ALU.add), vt, v)
            v = op("V", lambda e, buf=buf: e.reciprocal(buf, buf), v)
            v = op("V", lambda e, buf=buf, sl=sl: e.tensor_tensor(buf, acc[0:64, sl], buf, ALU.mult), v)
            v = op("V", lambda e, buf=buf, c=c, n=n: e.tensor_tensor(buf, buf, bank[c % 2][0:64, 0:n], ALU.add), v, pt)
            if kind == "mean":
                v = op("V", lambda e, buf=buf, sl=sl: e.tensor_scalar(hT[0:64, sl], buf, 0.0, None, ALU.max), v)
            elif kind == "mid":
                v = op("V", lambda e, buf=buf, buf2=buf2: e.tensor_scalar(buf2, buf, 0.0, pra[:, 0:1], ALU.min,
                                                                         ALU.mult), v)
                v = op("V", lambda e, buf=buf, buf2=buf2, sl=sl: e.scalar_tensor_tensor(
                    hT[0:64, sl], buf, 0.0, buf2, ALU.max, ALU.add), v)
            else:
                v = op("V", lambda e, buf=buf, sl=sl: e.tensor_copy(hT[0:64, sl], buf), v)
            op("V", lambda e, sl=sl: e.memset(acc[:, sl], 0.0))
            evs.append(v)
        return evs

    def add_rows(evs):
        bank = [pE[0], pE[1]]
        out = []
        for c in range(-(-NT // 8)):
            m = min(8, NT - 8 * c)
            for j in range(m):
                t = 8 * c + j
                w = [evs[t // 4]] + ([out[c - 2]] if c >= 2 else [])
                pt = op("P", lambda e, c=c, j=j, t=t: e.transpose(bank[c % 2][:, 64 * j:64 * j + 64],
                                                                  hT[0:64, 128 * t:128 * t + 128],
                                                                  ident[0:64, 0:64]), *w)
            out.append(op("V", lambda e, c=c, m=m: e.tensor_tensor(
                XR[:, 8 * c:8 * c + m, :], XR[:, 8 * c:8 * c + m, :],
                bank[c % 2][:, 0:64 * m].rearrange("p (t c) -> p t c", t=m), ALU.add), pt))
        return out

    spare = sem("spare")

    def edge_pass(name, kind, l, heads, start, qtab, kvtab, eat, ready):
        H, C = heads, 64 // heads
        scale = 1.0 / float(np.sqrt(np.float32(C)))
        att = kind == "att"
        if att:
            order = {
                "V": ["B flag", "B scan", "A O", "A last", "A cont", "B fw", "B cr", "A kj", "B pbm", "B X",
                      "B Mm", "B df", "A vj", "A prod", "B d", "A alpha", "B vals", "B facc", "B acc"],
                "P": ["B aT", "A e0", "A e1", "B Fb"] + [f"A OT{m}" for m in range(T)]
                     + [f"B Mn{j}" for j in range(T + 1)] + [f"A q{j}" for j in range(T)]
                     + [f"B Me{j}" for j in range(T)] + ["B fac"] + [f"B agg{j}" for j in range(T)],
                "A": ["A tb", "A OTs", "B fb", "B w"],
            }
        else:
            order = {
                "V": ["A O", "B acc"],
                "P": [f"A OT{m}" for m in range(T)] + [f"B agg{j}" for j in range(T)]
                     + ["A e0"] + [f"A q{j}" for j in range(T)],
                "A": ["A OTs", "A relu"],
            }
        prog = {k: sem(f"{name}_{k}") for k in "VPA"}
        s_i = [sem(f"{name}_i{u}") for u in range(3)]
        s_l = [sem(f"{name}_l{u}") for u in range(3)]
        s_g = [sem(f"{name}_g{u}") for u in range(3)]
        stage = {k: {o[2:]: o[0] for o in order[k]} for k in order}
        pos = {k: {o[2:]: n for n, o in enumerate(order[k])} for k in order}
        K = {k: len(order[k]) for k in order}
        NL = 4 if att else 2

        def val(k, o, s):
            t1 = s + 1 if stage[k][o] == "B" else s
            return (t1 + 3).times(3 * K[k], 0) + (t1.c % 3) * K[k] + pos[k][o] + 1

        def after(e, k, o, s):
            e.wait_ge(prog[k], val(k, o, s))

        def hold(e):
            e.sem_inc(spare, 1)

        def ge16(e, sems, per, s):
            e.wait_ge(sems[s.slot], s.times(16 * per, 16 * per))

        def v_O(e, s):
            u = s.slot
            ge16(e, s_i, 1, s)
            after(e, "P", "agg7", s - 3)
            return e.scalar_tensor_tensor(
                O[u][:, :, :], sdn[u][:, T:2 * T].unsqueeze(2).to_broadcast([128, T, W]),
                bf[:, bass.ds(s.value(), 1)],
                iof[:, 0:W].unsqueeze(1).to_broadcast([128, T, W]), ALU.subtract, ALU.is_equal)

        def v_last(e, s):
            u = s.slot
            after(e, "P", f"Mn{T}", s - 3)
            return e.tensor_tensor(fw[u][:, :, H:H + 1], sdn[u][:, T:2 * T].unsqueeze(2),
                                   sdn[u][:, 2 * T:3 * T].unsqueeze(2), ALU.not_equal)

        def v_cont(e, s):
            u, before = s.slot, (s - 1).slot
            if isinstance(s.i, int) and s.i == 0 and s.c == 0:
                return e.memset(cont[u][:, :], 0.0)
            return e.tensor_scalar(cont[u][:, :], sdn[before][:, 2 * T - 1:2 * T],
                                   bf[:, bass.ds(s.value(), 1)], None, ALU.is_equal)

        def v_kj(e, s):
            u = s.slot
            ge16(e, s_g, T, s)
            after(e, "P", "e1", s)
            after(e, "V", "alpha", s - 1)
            return e.tensor_tensor(kj[:, :, :], G[u][:, :, 0:64],
                                   pE[u][:, :].rearrange("p (j c) -> p j c", c=64), ALU.add)

        def v_vj(e, s):
            u = s.slot
            return e.tensor_tensor(vj[u][:, :, :], G[u][:, :, 64:128],
                                   pE[u][:, :].rearrange("p (j c) -> p j c", c=64), ALU.add)

        def v_prod(e, s):
            after(e, "V", "kj", s)
            after(e, "P", "q7", s)
            return e.tensor_tensor(kj[:, :, :], kj[:, :, :], pQ[:, :].rearrange("p (j c) -> p j c", c=64), ALU.mult)

        def v_alpha(e, s):
            u = s.slot
            after(e, "V", "prod", s)
            return e.tensor_reduce(al[u][:, 0:H * T].rearrange("p (h j) -> p j h", h=H),
                                   kj[:, :, :].rearrange("p j (h c) -> p j h c", h=H), AX.X, ALU.add)

        def v_flag(e, s):
            u = s.slot
            after(e, "A", "tb", s)
            after(e, "V", "scan", s - 1)
            return e.tensor_tensor(flg[0:H * T, 1:128], tb[u][0:H * T, 0:127], tb[u][0:H * T, 1:128], ALU.subtract)

        def v_scan(e, s):
            after(e, "V", "flag", s)
            after(e, "P", "aT", s)
            return e.tensor_tensor_scan(Fs[0:H * T, :], flg[0:H * T, :], pAT[0:H * T, :], -BIG, ALU.add, ALU.max)

        def v_fw(e, s):
            u = s.slot
            after(e, "P", "Fb", s)
            after(e, "V", "last", s)
            return e.tensor_tensor(fw[u][:, :, 0:H], pFb[:, 0:H * T].rearrange("p (h j) -> p j h", h=H),
                                   fw[u][:, :, H:H + 1].to_broadcast([128, T, H]), ALU.mult)

        def v_cr(e, s):
            u = s.slot
            after(e, "V", "cont", s)
            return e.tensor_scalar(cr[:, 0:H + 1], pMe[:, (T - 1) * (H + 1):T * (H + 1)], cont[u][:, 0:1], None,
                                   ALU.mult)

        pmn = pMn[:, 0:(T + 1) * (H + 1)].rearrange("p (j h) -> p j h", h=H + 1)
        pme = pMe[:, 0:T * (H + 1)].rearrange("p (j h) -> p j h", h=H + 1)

        def v_pbm(e, s):
            after(e, "P", f"Mn{T}", s)
            after(e, "V", "X", s - 1)
            return e.tensor_scalar(pbm[:, :], pmn[:, :, H], -1.0, BIG, ALU.add, ALU.mult)

        def v_X(e, s):
            after(e, "V", "pbm", s)
            return e.tensor_tensor(X[:, 0:H, :], pmn[:, :, 0:H].rearrange("p j h -> p h j"),
                                   pbm[:, :].unsqueeze(1).to_broadcast([W, H, T + 1]), ALU.add)

        def v_Mm(e, s):
            after(e, "V", "X", s)
            return e.tensor_reduce(Mm[:, 0:H], X[:, 0:H, :], AX.X, ALU.max)

        def v_df(e, s):
            after(e, "V", "Mm", s)
            return e.tensor_tensor(df[:, 0:H], X[:, 0:H, T], Mm[:, 0:H], ALU.subtract)

        def v_d(e, s):
            u = s.slot
            after(e, "P", "Me7", s)
            return e.tensor_tensor(dd[:, :, 0:H], al[u][:, 0:H * T].rearrange("p (h j) -> p j h", h=H),
                                   pme[:, :, 0:H], ALU.subtract)

        def v_vals(e, s):
            u = s.slot
            after(e, "A", "w", s)
            after(e, "V", "vj", s)
            return e.tensor_tensor(vals[u][:, :, 0:64], vj[u][:, :, :], vals[u][:, :, 64:128], ALU.mult)

        base_of = {}

        def v_facc(e, s):
            base_of[s.c] = e.value_load(tbl[0:1, 1, bass.ds(s.value(), 1)], min_val=0, max_val=z.idle)
            after(e, "P", "agg7", s)
            after(e, "V", "acc", s - 1)
            c = acc[:, bass.ds(base_of[s.c], 1)]
            return e.tensor_scalar(c, c, pFac, None, ALU.mult)

        def v_acc(e, s):
            if att:
                after(e, "V", "facc", s)
            else:
                base_of[s.c] = e.value_load(tbl[0:1, 1, bass.ds(s.value(), 1)], min_val=0, max_val=z.idle)
                after(e, "V", "acc", s - 1)
            after(e, "P", "agg7", s)
            c = acc[:, bass.ds(base_of[s.c], W)]
            return e.tensor_tensor(c, c, pG[:, 0:64], ALU.add)

        def p_e0(e, s):
            u = s.slot
            ge16(e, s_l, NL, s)
            if att:
                after(e, "V", "vj", s - 3)
                return e.matmul(pE[u][:, 0:256], ea[u][:, 0:128], bd32[:, l, :], start=True, stop=True)
            after(e, "A", "relu", s - 3)
            return e.matmul(pE[u][:, :], ea[u][:, 0:128], bd16[:, :], start=True, stop=False)

        def p_e1(e, s):
            u = s.slot
            return e.matmul(pE[u][:, 256:512], ea[u][:, 128:256], bd32[:, l, :], start=True, stop=True)

        def p_OT(e, s, m):
            u = s.slot
            if m == 0:
                after(e, "V", "O", s)
                after(e, "A", "OTs", s - 1)
                hold(e)
            return e.transpose(pOT[:, 128 * m:128 * m + 128], O[u][:, m, :], ident[:, :])

        def p_q(e, s, j):
            u = s.slot
            if j == 0:
                after(e, "A", "OTs", s)
                if att:
                    after(e, "V", "prod", s - 1)
            out = pQ if att else pE[u]
            return e.matmul(out[:, 64 * j:64 * j + 64], OTs[u][:, j, :], qw[u][:, :],
                            start=att, stop=att or j == T - 1)

        def p_aT(e, s):
            u = s.slot
            after(e, "V", "alpha", s)
            hold(e)
            return e.transpose(pAT[0:H * T, :], al[u][:, 0:H * T], ident[:, :])

        def p_Fb(e, s):
            after(e, "V", "scan", s)
            hold(e)
            return e.transpose(pFb[:, 0:H * T], Fs[0:H * T, :], ident[0:H * T, 0:H * T])

        def p_Mn(e, s, j):
            u = s.slot
            if j == 0:
                after(e, "V", "cr", s)
            lhs = cmat[:, :] if j == T else O[u][:, j, :]
            rhs = cr[:, 0:H + 1] if j == T else fw[u][:, j, 0:H + 1]
            return e.matmul(pmn[:, j, :], lhs, rhs, start=True, stop=True)

        def p_Me(e, s, j):
            u = s.slot
            if j == 0:
                after(e, "V", "Mm", s)
            return e.matmul(pme[:, j, :], OTs[u][:, j, :], Mm[:, 0:H + 1],
                            start=True, stop=True)

        def p_agg(e, s, j):
            u = s.slot
            if j == 0:
                if att:
                    after(e, "V", "vals", s)
                else:
                    after(e, "A", "relu", s)
                if not att:
                    after(e, "V", "acc", s - 1)
            return e.matmul(pG[:, 0:64], vals[u][:, j, :], O[u][:, j, :], start=j == 0, stop=j == T - 1)

        def p_fac(e, s):
            after(e, "A", "fb", s)
            after(e, "V", "acc", s - 1)
            return e.matmul(pFac, fb[:, :], e0[:, :], start=True, stop=True)

        def a_tb(e, s):
            u = s.slot
            ge16(e, s_l, NL, s)
            after(e, "V", "flag", s - 3)
            return e.activation(tb[u][0:H * T, :], dr[u][0:H * T, :], ACT.Copy, scale=BIG)

        def a_OTs(e, s):
            u = s.slot
            after(e, "P", "OT7", s)
            after(e, "P", "Me7" if att else "q7", s - 3)
            return e.activation(OTs[u][:, :, :], pOT[:, :].rearrange("p (a b) -> p a b", a=T), ACT.Copy)

        def a_fb(e, s):
            after(e, "V", "df", s)
            after(e, "P", "fac", s - 1)
            return e.activation(
                fb[:, :].rearrange("p (a h c) -> p a h c", a=2, h=H),
                df[:, 0:H].unsqueeze(1).unsqueeze(3).to_broadcast([64, 2, H, C]), ACT.Exp, scale=scale)

        def a_w(e, s):
            u = s.slot
            after(e, "V", "d", s)
            after(e, "P", "agg7", s - 3)
            return e.activation(vals[u][:, :, 64:128].rearrange("p j (h c) -> p j h c", h=H),
                                dd[:, :, 0:H].unsqueeze(3).to_broadcast([128, T, H, C]), ACT.Exp, scale=scale)

        def a_relu(e, s):
            u = s.slot
            after(e, "P", "q7", s)
            after(e, "P", "agg7", s - 3)
            return e.activation(vals[u][:, :, 0:64], pE[u][:, :].rearrange("p (j c) -> p j c", c=64), ACT.Relu)

        table = {"V": dict(O=v_O, last=v_last, cont=v_cont, kj=v_kj, vj=v_vj, prod=v_prod, alpha=v_alpha,
                           flag=v_flag, scan=v_scan, fw=v_fw, cr=v_cr, pbm=v_pbm, X=v_X, Mm=v_Mm, df=v_df,
                           d=v_d, vals=v_vals, facc=v_facc, acc=v_acc),
                 "P": dict(e0=p_e0, e1=p_e1, OT=p_OT, q=p_q, aT=p_aT, Fb=p_Fb, Mn=p_Mn, Me=p_Me, agg=p_agg,
                           fac=p_fac),
                 "A": dict(tb=a_tb, OTs=a_OTs, fb=a_fb, w=a_w, relu=a_relu)}

        def emit(e, k, t, stages):
            for n, o in enumerate(order[k]):
                if o[0] not in stages:
                    e.wait_ge(prog[k], (t + 4).times(3 * K[k], 0) + (t + 4).c % 3 * K[k] + n)
                    e.sem_inc(prog[k], 1)
                    continue
                s = t if o[0] == "B" else t + 1
                f = table[k].get(o[2:])
                if f is None:
                    part = o[2:].rstrip("0123456789")
                    table[k][part](e, s, int(o[2 + len(part):])).then_inc(prog[k], 1)
                else:
                    f(e, s).then_inc(prog[k], 1)

        def count_of(e):
            return e.value_load(ntr[0:1, 0:1], min_val=1, max_val=(SM - 1) // 3)

        def engine(k):
            def run(e):
                for w in start[k]:
                    e.wait_ge(*w)
                e.sem_inc(prog[k], 3 * K[k])
                n = count_of(e)
                emit(e, k, At(0, -1), "A")
                with e.Fori(0, n) as i:
                    for c in range(3):
                        emit(e, k, At(i, c), "AB")
                emit(e, k, At(n, 0), "B")
                e.wait_ge(prog[k], val_end(k, n))
                hold(e)
            return run

        def val_end(k, n):
            return n * (3 * K[k]) + 5 * K[k]

        def loads(e, s):
            u = s.slot
            b = e.value_load(tbl[0:1, 0, bass.ds(s.value(), 1)], min_val=0, max_val=B - 1)
            base = e.value_load(tbl[0:1, 1, bass.ds(s.value(), 1)], min_val=0, max_val=z.idle)
            after(e, "V", "cont" if att else "O", s - 2 if att else s - 3)
            e.dma_start(sdn[u][:, :], a["sdn"][bass.ds(b, 1)].rearrange("a p c -> (a p) c")).then_inc(s_i[u], 16)
            after(e, "P", "q7", s - 3)
            e.dma_start(ea[u][:, 0:eat.shape[2]], eat[bass.ds(b, 1)].rearrange("a p c -> (a p) c")).then_inc(s_l[u], 16)
            e.dma_start(qw[u][:, :], qtab[bass.ds(base, W), :]).then_inc(s_l[u], 16)
            if att:
                after(e, "A", "tb", s - 3)
                for h in range(2):
                    e.dma_start(dr[u][T * h:T * h + T, :],
                                a["dr"][bass.ds(b, 1)].rearrange("a p c -> (a p) c")).then_inc(s_l[u], 16)

        def sync(e):
            for w in ready:
                e.wait_ge(*w)
            n = count_of(e)
            loads(e, At(0, 0))
            with e.Fori(0, n) as i:
                for c in (1, 2, 3):
                    loads(e, At(i, c))

        def gathers(e, s):
            u = s.slot
            ge16(e, s_i, 1, s)
            hold(e)
            after(e, "V", "vj", s - 3)
            hold(e)
            for j in range(T):
                e.indirect_dma_start(G[u][:, j, :], None, kvtab,
                                     bass.IndirectOffsetOnAxis(ap=sdn[u][:, j:j + 1], axis=0)).then_inc(s_g[u], 16)

        def pool(e):
            for w in ready:
                e.wait_ge(*w)
            n = count_of(e)
            gathers(e, At(0, 0))
            with e.Fori(0, n) as i:
                for c in (1, 2, 3):
                    gathers(e, At(i, c))

        for k in "VPA":
            queue[k].append(engine(k))
        queue["S"].append(sync)
        if att:
            queue["G"].append(pool)

    evs = norm_rows(x_t)
    ready = tables(evs, 64, w1[:, :], [(PT, 0, 64)])
    vt = last("V")
    edge_pass("m", "mean", 0, 1, {"V": [t_t], "P": [w_t, vt], "A": [t_t]}, PT, None, a["ea16"], ready + [t_t])
    evs = fold("mean", 0, last("V"))
    out = add_rows(evs)
    evs = norm_rows(out[-1])
    for l in range(3):
        ready = tables(evs, 192, wkvq[:, l, :], [(KV[l], 0, 128), (QT[l], 128, 64)])
        vt = op("V", lambda e: e.memset(Mm[:, :], 1.0))
        edge_pass(f"a{l}", "att", l, 2 if l < 2 else 1, {"V": [], "P": [vt], "A": [vt]},
                  QT[l], KV[l], a["ea32"], ready + [t_t])
        evs = fold("mid" if l < 2 else "last", l, last("V"))
    out = add_rows(evs)
    s_o = sem("s_o")
    full = N // 128
    o1 = dma("S", s_o, 16, lambda e: e.dma_start(
        a["out"][0:128 * full, :].rearrange("(t p) c -> p t c", p=128), XR[:, 0:full, :]), out[-1])
    if N % 128:
        o1 = dma("S", s_o, 32, lambda e: e.dma_start(a["out"][128 * full:N, :], XR[0:N % 128, full, :]))
    queue["S"].append(lambda e: e.wait_ge(*o1))

    block = ctx.enter_context(nc.Block())

    @block.sync
    def _(e):
        for f in queue["S"]:
            f(e)

    @block.gpsimd
    def _(e):
        for f in queue["G"]:
            f(e)

    @block.scalar
    def _(e):
        for f in queue["A"]:
            f(e)

    @block.vector
    def _(e):
        for f in queue["V"]:
            f(e)

    @block.tensor
    def _(e):
        for f in queue["P"]:
            f(e)


def layout(x, src, dst, edge_attr_16, edge_attr_32, z):
    ep = z.blocks * BE
    out = {}
    xp = np.zeros((z.nc, 64), np.float32)
    xp[:z.n] = x
    out["x"] = xp
    s = np.zeros(ep, np.int32)
    s[:z.e] = src
    d = np.full(ep, z.n, np.int32)
    d[:z.e] = dst
    s3 = s.reshape(z.blocks, T, 128)
    d3 = d.reshape(z.blocks, T, 128)
    nx = np.full((z.blocks, T, 128), -1, np.int32)
    nx[:, :, :127] = d3[:, :, 1:]
    out["sdn"] = np.ascontiguousarray(np.concatenate([s3, d3, nx], axis=1).transpose(0, 2, 1))
    out["dr"] = np.ascontiguousarray(d3)
    dfl = d.reshape(z.blocks, BE)
    out["dst_first"] = np.ascontiguousarray(dfl[:, 0]).reshape(1, -1)
    out["dst_last"] = np.ascontiguousarray(dfl[:, -1]).reshape(1, -1)
    e16 = np.zeros((ep, 16), np.float32)
    e16[:z.e] = edge_attr_16
    out["ea16"] = np.ascontiguousarray(e16.reshape(z.blocks, T, 128, 16).transpose(0, 1, 3, 2)).reshape(
        z.blocks, T * 16, 128)
    e32 = np.zeros((ep, 32), np.float32)
    e32[:z.e] = edge_attr_32
    out["ea32"] = np.ascontiguousarray(e32.reshape(z.blocks, 2, 4, 128, 32).transpose(0, 2, 4, 1, 3)).reshape(
        z.blocks, 128, 256)
    return out


def arrays_of(inputs, z):
    out = layout(*(np.asarray(inputs[k]) for k in ("x", "src", "dst", "edge_attr_16", "edge_attr_32")), z)
    for k in ("W1", "b1", "Wres", "bres"):
        out[k] = np.asarray(inputs["L0_gnn_" + k])
    for l in range(3):
        for k in ("Wq", "bq", "Wk", "bk", "Wv", "bv", "We", "Ws", "bs"):
            out[f"{k}{l}"] = np.asarray(inputs[f"L1_gnn_{k}{l}"])
    out["prelu"] = np.asarray(inputs["L1_gnn_prelu_a"]).reshape(1)
    return out


def kernel(**inputs):
    import concourse.bacc as bacc
    from concourse.bass_utils import run_bass_kernel_spmd

    z = Sizes(inputs["x"].shape[0], inputs["src"].shape[0])
    arrays = arrays_of(inputs, z)
    nc = bacc.Bacc("TRN2", target_bir_lowering=False, num_devices=1)
    a = {k: nc.dram_tensor(f"in_{k}", v.shape, mybir.dt.from_np(v.dtype), kind="ExternalInput").ap()
         for k, v in arrays.items()}
    a["out"] = nc.dram_tensor("out_0", (z.n, 64), F32, kind="ExternalOutput").ap()
    gnn_program(nc, z, a)
    r = run_bass_kernel_spmd(nc, [{f"in_{k}": v for k, v in arrays.items()}], core_ids=[0])
    return r.results[0]["out_0"]
```

```python
import numpy as np
from contextlib import ExitStack

import concourse.bass as bass
from concourse import mybir

F32 = mybir.dt.float32
I32 = mybir.dt.int32
BF16 = mybir.dt.bfloat16
ALU = mybir.AluOpType
ACT = mybir.ActivationFunctionType
AX = mybir.AxisListType
BIG = 1.0e30
EPS = 1e-5

T = 8
BE = 128 * T
BIAS = 6
W = 64


class Sizes:
    def __init__(self, n, e):
        self.n = n
        self.e = e
        self.blocks = -(-e // BE)
        self.blocks += self.blocks % 2
        self.tiles = -(-(n + 1 + W) // 128)
        self.nc = self.tiles * 128
        self.idle = n + 1
        self.peel = (self.blocks - 3) % 3
        self.smax = W + self.blocks + -(-(n + 1) // W) + 3 + 3
        assert self.idle + W <= self.nc and self.smax <= 512


class At:

    def __init__(self, i, c):
        self.i, self.c = i, c

    def __add__(self, d):
        return At(self.i, self.c + d)

    def __sub__(self, d):
        return At(self.i, self.c - d)

    @property
    def slot(self):
        return self.c % 3

    def times(self, k, add):
        return self.i * k + (self.c // 3 * k + add)

    def value(self):
        return self.i * 3 + self.c


def gnn_program(nc, z, a):
    ctx = ExitStack()
    with ctx:
        build(nc, z, a, ctx)


def build(nc, z, a, ctx):
    B, NCOL, NT, SM = z.blocks, z.nc, z.tiles, z.smax
    N = z.n

    def sb(name, shape, dt=F32):
        return ctx.enter_context(nc.sbuf_tensor(name, shape, dt))

    def pb(name, shape, dt=F32):
        return ctx.enter_context(nc.psum_tensor(name, shape, dt))

    def sem(name):
        return ctx.enter_context(nc.semaphore(name))

    XR = sb("XR", [128, NT, 64])
    WK = sb("WK", [128, NT, 64])
    hT = sb("hT", [65, NCOL])
    acc = sb("acc", [66, NCOL])
    SQ = sb("SQ", [128, NT, 64])
    st = sb("st", [128, 4, NT])
    w1 = sb("w1", [65, 64])
    wr = sb("wr", [65, 64])
    bd16 = sb("bd16", [128, T * 64])
    wkvq = sb("wkvq", [65, 3, 192])
    bd32 = sb("bd32", [128, 3, 256])
    wskip = sb("wskip", [65, 3, 64])
    pra = sb("pra", [64, 1])
    ident = sb("ident", [128, 128])
    cmat = sb("cmat", [128, W])
    cmb = sb("cmb", [128, W], BF16)
    idb = sb("idb", [128, 128], BF16)
    sel = sb("sel", [66, 2, 64])
    e0 = sb("e0", [64, 1])
    ioi = sb("ioi", [128, SM], I32)
    iof = sb("iof", [128, SM])
    bf = sb("bf", [128, SM])
    tbl = sb("tbl", [128, 2, SM], I32)
    ntr = sb("ntr", [128, 1], I32)
    fl = sb("fl", [1, 2, B], I32)
    flf = sb("flf", [1, 2, B])
    wi = sb("wi", [1, 2, B], I32)
    pe_ = sb("pe_", [1, 4, B + 1])
    pcol = sb("pcol", [128, 2, 2])
    cmp_ = sb("cmp_", [128, 2, SM])
    dlh = sb("dlh", [128, 2, 128])
    ones = sb("ones", [128, 128])
    n3 = sb("n3", [1, 2, SM])
    fbuf = sb("fbuf", [64, 2, 512])
    stg = sb("stg", [128, 2, 4, 192])
    stq = sb("stq", [128, 2, 4, 192], BF16)
    rq = sb("rq", [128, 4, 64])

    G = [sb(f"G{u}", [128, T, 128]) for u in range(3)]
    sdn = [sb(f"sdn{u}", [128, 3 * T], I32) for u in range(3)]
    ea = [sb(f"ea{u}", [128, 256]) for u in range(3)]
    dr = [sb(f"dr{u}", [16, 128], I32) for u in range(3)]
    qw = [sb(f"qw{u}", [W, 192], BF16) for u in range(3)]
    O = [sb(f"O{u}", [128, T, W]) for u in range(3)]
    Ob = [sb(f"Ob{u}", [128, T, W], BF16) for u in range(3)]
    OTs = [sb(f"OTs{u}", [W, T, 128], BF16) for u in range(3)]
    kj = sb("kj", [128, T, 64])
    vj = [sb(f"vj{u}", [128, T, 64]) for u in range(3)]
    vals = [sb(f"vals{u}", [128, T, 66]) for u in range(3)]
    al = [sb(f"al{u}", [128, 2 * T]) for u in range(3)]
    tb = [sb(f"tb{u}", [16, 128]) for u in range(3)]
    flg = [sb(f"flg{u}", [16, 128]) for u in range(3)]
    Fs = sb("Fs", [16, 128])
    fw = [sb(f"fw{u}", [128, T, 8], BF16) for u in range(3)]
    cont = [sb(f"cont{u}", [128, 1]) for u in range(3)]
    cr = sb("cr", [128, 8], BF16)
    fm = sb("fm", [128, T, 2])
    pbm = sb("pbm", [W, T + 1])
    X = sb("X", [W, 2, T + 1])
    Mm = sb("Mm", [W, 2])
    Mb = sb("Mb", [W, 8], BF16)
    X1 = sb("X1", [W, 2, T + 1])
    d1 = sb("d1", [128, T, 2])
    df = sb("df", [W, 2])
    fb = sb("fb", [W, 66])
    dd = sb("dd", [128, T, 2])

    pE = [pb(f"pE{u}", [128, T * 64]) for u in range(3)]
    pOT = pb("pOT", [W, T * 128], BF16)
    pY = pb("pY", [128, 512])
    pQ = pb("pQ", [128, 512])
    pS = pb("pS", [128, 512])
    pG = pb("pG", [128, 512])
    pAT = pS[0:16, 0:128]
    pFb = pS[:, 128:144]
    pMn = pS[0:W, 160:160 + 5 * (T + 1)]
    pMe = pS[:, 256:256 + 5 * T]
    pFac = pG[0:66, 64:65]

    def dram(name, shape, dt=F32):
        return nc.dram_tensor(name, shape, dt, kind="Internal").ap()

    PT = dram("PT", [NCOL, 192], BF16)
    KV = [dram(f"KV{l}", [NCOL, 128]) for l in range(3)]
    QT = [dram(f"QT{l}", [NCOL, 192], BF16) for l in range(3)]

    queue = {k: [] for k in "VAPGS"}
    done = {k: sem(f"done_{k}") for k in "VAPG"}
    count = dict.fromkeys("VAPG", 0)

    def op(k, f, *waits):
        count[k] += 1

        def run(e):
            for s, v in waits:
                e.wait_ge(s, v)
            f(e).then_inc(done[k], 1)
        queue[k].append(run)
        return done[k], count[k]

    def dma(k, s, n, f, *waits):
        def run(e):
            for q, v in waits:
                e.wait_ge(q, v)
            f(e).then_inc(s, 16)
        queue[k].append(run)
        return s, n

    def last(k):
        return done[k], count[k]

    s_w = sem("s_w")
    nw = [0]

    def load(out, src, k="S"):
        nw[0] += 16
        dma(k, s_w, nw[0], lambda e, out=out, src=src: e.dma_start(out, src))

    def row(v, m):
        return v.rearrange("(a m) -> a m", a=1) if m else v

    s_x = sem("s_x")
    s_fl = sem("s_fl")
    x_t = dma("S", s_x, 16, lambda e: e.dma_start(XR[:, :, :], a["x"].rearrange("(t p) c -> p t c", p=128)))
    dma("A", s_fl, 16, lambda e: e.dma_start(fl[:, 0, :], a["dst_first"]))
    fl_t = dma("A", s_fl, 32, lambda e: e.dma_start(fl[:, 1, :], a["dst_last"]))

    zb = op("V", lambda e: e.memset(bd16[:, :], 0.0))
    zb2 = op("V", lambda e: e.memset(bd32[:, :, :], 0.0))
    queue["S"].append(lambda e: e.wait_ge(*zb2))
    load(w1[0:64, :], a["W1"][0:64, :])
    load(w1[64:65, :], row(a["b1"], 1))
    load(wr[0:64, :], a["Wres"])
    load(wr[64:65, :], row(a["bres"], 1))
    for j in range(T):
        load(bd16[16 * j:16 * j + 16, 64 * j:64 * j + 64], a["W1"][64:80, :])
    for l in range(3):
        for m, c in enumerate("kvq"):
            load(wkvq[0:64, l, 64 * m:64 * m + 64], a[f"W{c}{l}"])
            load(wkvq[64:65, l, 64 * m:64 * m + 64], row(a[f"b{c}{l}"], 1))
        for j in range(4):
            load(bd32[32 * j:32 * j + 32, l, 64 * j:64 * j + 64], a[f"We{l}"])
        load(wskip[0:64, l, :], a[f"Ws{l}"])
        load(wskip[64:65, l, :], row(a[f"bs{l}"], 1))
    load(pra[:, :], a["prelu"].rearrange("(a m) -> a m", a=1).to_broadcast([64, 1]))
    w_t = (s_w, nw[0])

    op("G", lambda e: e.memset(ident[:, :], 0.0))
    op("G", lambda e: e.memset(cmat[:, :], 0.0))
    op("G", lambda e: e.memset(e0[:, :], 0.0))
    g0 = op("G", lambda e: e.memset(ones[:, :], 1.0))
    op("G", lambda e: e.affine_select(out=ident[:, :], in_=ident[:, :], compare_op=ALU.not_equal, fill=1.0,
                                      base=0, pattern=[[-1, 128]], channel_multiplier=1), g0)
    op("G", lambda e: e.affine_select(out=cmat[:, :], in_=cmat[:, :], compare_op=ALU.not_equal, fill=1.0,
                                      base=-127, pattern=[[128, W]], channel_multiplier=1))
    op("G", lambda e: e.affine_select(out=e0[:, :], in_=e0[:, :], compare_op=ALU.not_equal, fill=1.0,
                                      base=0, pattern=[[1, 1]], channel_multiplier=1))
    op("G", lambda e: e.iota(ioi[:, :], pattern=[[1, SM]], base=0, channel_multiplier=0))
    op("G", lambda e: e.memset(sel[:, :, :], 1.0))
    gs = last("G")
    op("G", lambda e: e.affine_select(out=sel[:, 0, :], in_=sel[:, 0, :], compare_op=ALU.is_equal, fill=0.0,
                                      base=-64, pattern=[[0, 64]], channel_multiplier=1), gs)
    op("G", lambda e: e.affine_select(out=sel[:, 1, :].rearrange("p (a b) -> p a b", a=2),
                                      in_=sel[:, 1, :].rearrange("p (a b) -> p a b", a=2),
                                      compare_op=ALU.is_equal, fill=0.0,
                                      base=-64, pattern=[[-1, 2], [0, 32]], channel_multiplier=1), gs)
    g_t = last("G")
    op("V", lambda e: e.tensor_copy(cmb[:, :], cmat[:, :]), g_t)
    op("V", lambda e: e.tensor_copy(idb[:, :], ident[:, :]), g_t)
    io_t = op("V", lambda e: e.tensor_copy(iof[:, :], ioi[:, :]), g_t)

    op("V", lambda e: e.tensor_copy(flf[:, :, :], fl[:, :, :]), fl_t)
    v = op("V", lambda e: e.tensor_tensor(wi[:, 0, :], fl[:, 1, :], fl[:, 0, :], ALU.subtract))
    v = op("V", lambda e: e.tensor_scalar(wi[:, 1, :], wi[:, 0, :], 6, None, ALU.arith_shift_right), v)
    v = op("V", lambda e: e.memset(pe_[:, :, :], 0.0), v)
    v = op("V", lambda e: e.memset(pe_[:, 3, :], 1.0), v)
    v = op("V", lambda e: e.tensor_copy(pe_[:, 0, 0:B], wi[:, 1, :]), v)
    v = op("V", lambda e: e.tensor_scalar(pe_[:, 0, 0:B], pe_[:, 0, 0:B], 1.0, None, ALU.add), v)
    v = op("V", lambda e: e.tensor_tensor_scan(pe_[:, 1, 1:B + 1], pe_[:, 3, 0:B], pe_[:, 0, 0:B], 0.0,
                                               ALU.mult, ALU.add), v)
    v = op("V", lambda e: e.scalar_tensor_tensor(pe_[:, 2, 0:B], pe_[:, 1, 0:B], -float(W), flf[:, 0, :],
                                                 ALU.mult, ALU.add), v)
    v = op("V", lambda e: e.tensor_tensor(pe_[:, 0, 0:B - 1], pe_[:, 2, 1:B], pe_[:, 2, 0:B - 1], ALU.subtract), v)
    v = op("V", lambda e: e.memset(pe_[:, 0, B - 1:B], 0.0), v)
    HB = B // 2
    for k in range(2):
        op("P", lambda e, k=k: e.matmul(pQ[0:HB, k:k + 1], pe_[:, 1, 1 + k:B + 1:2], ones[0:1, 0:1],
                                        start=True, stop=True), v, g_t)
        op("P", lambda e, k=k: e.matmul(pQ[0:HB, 2 + k:3 + k], pe_[:, 0, k:B:2], ones[0:1, 0:1],
                                        start=True, stop=True))
    p = op("P", lambda e: e.matmul(pQ[:, 4:5], ones[0:1, :], flf[:, 0, 0:1], start=True, stop=True))
    v = op("V", lambda e: e.tensor_copy(pcol[0:HB, :, :], pQ[0:HB, 0:4].rearrange("p (a b) -> p a b", a=2)), p)
    f0 = sb("f0", [128, 1])
    op("V", lambda e: e.tensor_copy(f0[:, :], pQ[:, 4:5]))
    for k in range(2):
        op("V", lambda e, k=k: e.tensor_scalar(cmp_[0:HB, k, :], iof[0:HB, :], pcol[0:HB, 0, k:k + 1], None,
                                               ALU.is_ge), v)
        v2 = op("V", lambda e, k=k: e.tensor_scalar(dlh[0:HB, k, :], ones[0:HB, :], pcol[0:HB, 1, k:k + 1], None,
                                                    ALU.mult))
    for k in range(2):
        op("P", lambda e, k=k: e.matmul(pS[:, 0:SM], ones[0:HB, :], cmp_[0:HB, k, :],
                                        start=k == 0, stop=k == 1), v2)
    for k in range(2):
        p = op("P", lambda e, k=k: e.matmul(pG[:, 0:SM], dlh[0:HB, k, :], cmp_[0:HB, k, :],
                                            start=k == 0, stop=k == 1))
    idle = float(z.idle)
    v = op("V", lambda e: e.scalar_tensor_tensor(bf[:, :], iof[:, :], float(W), pG[:, 0:SM], ALU.mult, ALU.add), p)
    v = op("V", lambda e: e.tensor_scalar(bf[:, :], bf[:, :], f0[:, 0:1], idle, ALU.add, ALU.min), v)
    v3 = op("V", lambda e: e.tensor_scalar(cmp_[:, 0, :], pS[:, 0:SM], float(B), idle, ALU.is_ge, ALU.mult), v)
    v = op("V", lambda e: e.tensor_tensor(bf[:, :], bf[:, :], cmp_[:, 0, :], ALU.max), v3)
    op("V", lambda e: e.tensor_copy(tbl[:, 1, :], bf[:, :]), v)
    op("V", lambda e: e.tensor_scalar(tbl[:, 0, :], pS[:, 0:SM], float(B - 1), None, ALU.min))
    v = op("V", lambda e: e.tensor_scalar(n3[:, 0, :], iof[0:1, :], 3.0, 4.0 + z.peel, ALU.mult, ALU.add))
    v = op("V", lambda e: e.tensor_scalar(n3[:, 0, :], n3[:, 0, :], pe_[:, 1, B:B + 1], None, ALU.is_le), v)
    v = op("V", lambda e: e.tensor_reduce(n3[:, 1, 0:1], n3[:, 0, :], AX.X, ALU.add), v)
    t_t = op("V", lambda e: e.tensor_copy(ntr[0:1, :], n3[:, 1, 0:1]), v)
    op("V", lambda e: e.memset(hT[64:65, :], 1.0))
    op("V", lambda e: e.memset(pMe, 0.0))
    op("V", lambda e: e.memset(acc[:, :], 0.0))
    for u in range(3):
        op("V", lambda e, u=u: e.memset(flg[u][:, :], 0.0))
        op("V", lambda e, u=u: e.memset(vals[u][:, :, 64:66], 1.0))

    def norm_rows(xt):
        bank = [pQ, pY]
        v = op("V", lambda e: e.tensor_reduce(st[:, 0, :], XR[:, :, :], AX.X, ALU.add), xt)
        v = op("V", lambda e: e.tensor_scalar(st[:, 0, :], st[:, 0, :], 1.0 / 64, None, ALU.mult), v)
        v = op("V", lambda e: e.tensor_tensor(WK[:, :, :], XR[:, :, :], st[:, 0, :].unsqueeze(2).to_broadcast(
            [128, NT, 64]), ALU.subtract), v)
        sq = SQ[:, :, :]
        v = op("V", lambda e: e.tensor_tensor(sq, WK[:, :, :], WK[:, :, :], ALU.mult), v)
        v = op("V", lambda e: e.tensor_reduce(st[:, 1, :], sq, AX.X, ALU.add), v)
        v = op("V", lambda e: e.tensor_scalar(st[:, 1, :], st[:, 1, :], 1.0 / 64, EPS, ALU.mult, ALU.add), v)
        s = op("A", lambda e: e.activation(st[:, 2, :], st[:, 1, :], ACT.Sqrt), v)
        v = op("V", lambda e: e.reciprocal(st[:, 3, :], st[:, 2, :]), s)
        v = op("V", lambda e: e.tensor_tensor(WK[:, :, :], WK[:, :, :], st[:, 3, :].unsqueeze(2).to_broadcast(
            [128, NT, 64]), ALU.mult), v)
        evs = []
        for c in range(-(-NT // 4)):
            m = min(4, NT - 4 * c)
            for j in range(m):
                w = [v, g_t] if c < 2 else [evs[c - 2]]
                pt = op("P", lambda e, c=c, j=j: e.transpose(bank[c % 2][0:64, 128 * j:128 * j + 128],
                                                             WK[:, 4 * c + j, :], ident[:, :]), *w)
            evs.append(op("A", lambda e, c=c, m=m: e.activation(
                hT[0:64, 512 * c:512 * c + 128 * m], bank[c % 2][0:64, 0:128 * m], ACT.Relu), pt))
        return evs

    s_t = [sem(f"s_t{l}") for l in range(2)]
    nt = [0, 0]

    def tables(evs, lhs_n, weights, kv, qt):
        bank = [pE[0], pE[1]]
        free, qs = [], []
        nt0 = nt[0]
        for c in range(-(-NT // 2)):
            m = min(2, NT - 2 * c)
            g = (c // 2) % 2
            for j in range(m):
                w = [evs[c // 2]] + ([free[c - 2]] if c >= 2 else [w_t])
                pt = op("P", lambda e, c=c, j=j: e.matmul(
                    bank[c % 2][:, lhs_n * j:lhs_n * j + lhs_n], hT[:, 256 * c + 128 * j:256 * c + 128 * j + 128],
                    weights, start=True, stop=True), *w)
            w = [pt] + ([(s_t[g], nt[g])] if c % 2 == 0 and nt[g] else [])
            if c % 2 == 0 and len(qs) > 1:
                w.append(qs[-2])
            ev = op("A", lambda e, c=c, m=m, g=g: e.activation(
                stg[:, g, 2 * (c % 2):2 * (c % 2) + m, 0:lhs_n],
                bank[c % 2][:, 0:lhs_n * m].rearrange("p (t c) -> p t c", t=m), ACT.Copy), *w)
            free.append(ev)
            if c % 2 == 1 or 2 * c + m >= NT:
                t0, tn = 4 * (c // 2), min(4, NT - 4 * (c // 2))
                if kv is not None:
                    nt[g] += 16
                    dma("S", s_t[g], nt[g], lambda e, t0=t0, tn=tn, g=g: e.dma_start(
                        kv[128 * t0:128 * (t0 + tn), :].rearrange("(t p) c -> p t c", p=128),
                        stg[:, g, 0:tn, 0:128]), ev)
                src = stg[:, g, 0:tn, lhs_n - 64:lhs_n]
                hi, mi, lo = (stq[:, g, 0:tn, 64 * k:64 * k + 64] for k in range(3))
                rr = rq[:, 0:tn, :]
                w = [ev] + ([(s_t[g], nt[g] - 16 * (kv is not None))] if c > 3 or nt0 else [])
                v = op("V", lambda e, a=hi, b=src: e.tensor_copy(a, b), *w)
                v = op("V", lambda e, a=rr, b=src, c_=hi: e.tensor_tensor(a, b, c_, ALU.subtract), v)
                v = op("V", lambda e, a=mi, b=rr: e.tensor_copy(a, b), v)
                v = op("V", lambda e, a=lo, b=rr, c_=mi: e.tensor_tensor(a, b, c_, ALU.subtract), v)
                qs.append(v)
                nt[g] += 16
                dma("S", s_t[g], nt[g], lambda e, t0=t0, tn=tn, g=g: e.dma_start(
                    qt[128 * t0:128 * (t0 + tn), :].rearrange("(t p) c -> p t c", p=128),
                    stq[:, g, 0:tn, :]), v)
        return [(s_t[0], nt[0]), (s_t[1], nt[1])]

    def fold(kind, l, rows):
        bank = [pQ, pY]
        bank2 = [pS, pG]
        vt = op("V", lambda e: e.memset(pbm[:, :], 0.0))
        evs = []
        lhs = wr[:, :] if kind == "mean" else wskip[:, l, :]
        for c in range(-(-NCOL // 512)):
            n = min(512, NCOL - 512 * c)
            sl = slice(512 * c, 512 * c + n)
            wc = slice(0, n)
            buf = fbuf[:, 0, 0:n]
            buf2 = fbuf[:, 1, 0:n]
            w = [w_t, vt] if c < 2 else [evs[c - 2]]
            pt = op("P", lambda e, c=c, sl=sl, n=n: e.matmul(bank[c % 2][0:64, 0:n], lhs, hT[:, sl],
                                                             start=True, stop=True), *w)
            pd = op("P", lambda e, c=c, sl=sl, n=n: e.matmul(bank2[c % 2][0:64, 0:n], sel[0:rows, rows - 65, :],
                                                             acc[0:rows, sl], start=True, stop=True))
            v = last("V")
            if kind == "mean":
                v = op("V", lambda e, c=c, n=n, buf=buf: e.tensor_scalar(buf, bank2[c % 2][0:64, 0:n], 1.0, None,
                                                                         ALU.max), vt, v, pd)
            else:
                v = op("V", lambda e, c=c, n=n, buf=buf: e.tensor_scalar(buf, bank2[c % 2][0:64, 0:n], 1e-16, None,
                                                                         ALU.add), vt, v, pd)
            v = op("V", lambda e, buf=buf: e.reciprocal(buf, buf), v)
            v = op("V", lambda e, buf=buf, sl=sl: e.tensor_tensor(buf, acc[0:64, sl], buf, ALU.mult), v)
            v = op("V", lambda e, buf=buf, c=c, n=n: e.tensor_tensor(buf, buf, bank[c % 2][0:64, 0:n], ALU.add), v, pt)
            if kind == "mean":
                v = op("V", lambda e, buf=buf, sl=sl: e.tensor_scalar(hT[0:64, sl], buf, 0.0, None, ALU.max), v)
            elif kind == "mid":
                v = op("V", lambda e, buf=buf, buf2=buf2: e.tensor_scalar(buf2, buf, 0.0, pra[:, 0:1], ALU.min,
                                                                         ALU.mult), v)
                v = op("V", lambda e, buf=buf, buf2=buf2, sl=sl: e.scalar_tensor_tensor(
                    hT[0:64, sl], buf, 0.0, buf2, ALU.max, ALU.add), v)
            else:
                v = op("V", lambda e, buf=buf, sl=sl: e.tensor_copy(hT[0:64, sl], buf), v)
            op("V", lambda e, sl=sl: e.memset(acc[:, sl], 0.0))
            evs.append(v)
        return evs

    def add_rows(evs):
        bank = [pE[0], pE[1]]
        out = []
        for c in range(-(-NT // 8)):
            m = min(8, NT - 8 * c)
            for j in range(m):
                t = 8 * c + j
                w = [evs[t // 4]] + ([out[c - 2]] if c >= 2 else [])
                pt = op("P", lambda e, c=c, j=j, t=t: e.transpose(bank[c % 2][:, 64 * j:64 * j + 64],
                                                                  hT[0:64, 128 * t:128 * t + 128],
                                                                  ident[0:64, 0:64]), *w)
            out.append(op("V", lambda e, c=c, m=m: e.tensor_tensor(
                XR[:, 8 * c:8 * c + m, :], XR[:, 8 * c:8 * c + m, :],
                bank[c % 2][:, 0:64 * m].rearrange("p (t c) -> p t c", t=m), ALU.add), pt))
        return out

    spare = sem("spare")

    def edge_pass(name, kind, l, heads, start, qtab, kvtab, eat, ready):
        H, C = heads, 64 // heads
        scale = 1.0 / float(np.sqrt(np.float32(C)))
        att = kind == "att"
        AR = 64 + H
        if att:
            order = {
                "V": ["B scan", "A cont", "A last", "B fm", "B fhi", "B flo", "B cr", "A kj", "B pbm",
                      "B X1", "B X", "B Mm", "B Mhi", "B Mlo", "B df", "A vj", "B d1", "B d", "A prod",
                      "B vals", "A alpha", "A flag", "C facc", "C acc", "Z O"],
                "P": ["B Fb"] + [f"A OT{m}" for m in range(T)] + [f"B Mn{j}" for j in range(T + 1)]
                     + ["C fac"] + [f"C agg{j}" for j in range(5)] + [f"B Me{j}" for j in range(T)]
                     + [f"C agg{j}" for j in range(5, T)] + [f"A q{j}" for j in range(3 * T)]
                     + ["Z e0", "Z e1", "A aT"],
                "A": ["A tb", "A OTs", "B fb", "B fbw", "B w", "Z Ob"],
            }
        else:
            order = {
                "V": ["Z O", "C acc"],
                "P": ["A e0"] + [f"A q{j}" for j in range(3 * T)] + [f"Z OT{m}" for m in range(T)]
                     + [f"B agg{j}" for j in range(T)],
                "A": ["Z Ob", "A relu", "Z OTs"],
            }
        lead = {"Z": 2, "A": 1, "B": 0, "C": -1}
        prog = {k: sem(f"{name}_{k}") for k in "VPA"}
        s_i = [sem(f"{name}_i{u}") for u in range(3)]
        s_l = [sem(f"{name}_l{u}") for u in range(3)]
        s_g = [sem(f"{name}_g{u}") for u in range(3)]
        stage = {k: {o[2:]: o[0] for o in order[k]} for k in order}
        pos = {k: {o[2:]: n for n, o in enumerate(order[k])} for k in order}
        K = {k: len(order[k]) for k in order}
        NL = 4 if att else 2

        def val(k, o, s):
            t4 = s + (BIAS - lead[stage[k][o]])
            return t4.times(3 * K[k], 0) + (t4.c % 3) * K[k] + pos[k][o] + 1

        def after(e, k, o, s):
            e.wait_ge(prog[k], val(k, o, s))

        def hold(e):
            e.sem_inc(spare, 1)

        def ge16(e, sems, per, s):
            e.wait_ge(sems[s.slot], s.times(16 * per, 16 * per))

        def v_O(e, s):
            u = s.slot
            ge16(e, s_i, 1, s)
            after(e, "P", "agg7", s - 3)
            return e.scalar_tensor_tensor(
                O[u][:, :, :], sdn[u][:, T:2 * T].unsqueeze(2).to_broadcast([128, T, W]),
                bf[:, bass.ds(s.value(), 1)],
                iof[:, 0:W].unsqueeze(1).to_broadcast([128, T, W]), ALU.subtract, ALU.is_equal)

        def v_last(e, s):
            u = s.slot
            after(e, "P", f"Mn{T}", s - 3)
            return e.tensor_tensor(fw[u][:, :, 2 * H:2 * H + 1], sdn[u][:, T:2 * T].unsqueeze(2),
                                   sdn[u][:, 2 * T:3 * T].unsqueeze(2), ALU.not_equal)

        def v_cont(e, s):
            u, before = s.slot, (s - 1).slot
            if isinstance(s.i, int) and s.i == 0 and s.c == 0:
                return e.memset(cont[u][:, :], 0.0)
            return e.tensor_scalar(cont[u][:, :], sdn[before][:, 2 * T - 1:2 * T],
                                   bf[:, bass.ds(s.value(), 1)], None, ALU.is_equal)

        def v_kj(e, s):
            u = s.slot
            ge16(e, s_g, T, s)
            after(e, "P", "e1", s)
            after(e, "V", "alpha", s - 1)
            return e.tensor_tensor(kj[:, :, :], G[u][:, :, 0:64],
                                   pE[u][:, :].rearrange("p (j c) -> p j c", c=64), ALU.add)

        def v_vj(e, s):
            u = s.slot
            return e.tensor_tensor(vj[u][:, :, :], G[u][:, :, 64:128],
                                   pE[u][:, :].rearrange("p (j c) -> p j c", c=64), ALU.add)

        def v_prod(e, s):
            after(e, "V", "kj", s)
            after(e, "P", "q23", s)
            return e.tensor_tensor(kj[:, :, :], kj[:, :, :], pQ[:, :].rearrange("p (j c) -> p j c", c=64), ALU.mult)

        def v_alpha(e, s):
            u = s.slot
            after(e, "V", "prod", s)
            return e.tensor_reduce(al[u][:, 0:H * T].rearrange("p (h j) -> p j h", h=H),
                                   kj[:, :, :].rearrange("p j (h c) -> p j h c", h=H), AX.X, ALU.add)

        def v_flag(e, s):
            u = s.slot
            after(e, "A", "tb", s)
            return e.tensor_tensor(flg[u][0:H * T, 1:128], tb[u][0:H * T, 0:127], tb[u][0:H * T, 1:128],
                                   ALU.subtract)

        def v_scan(e, s):
            u = s.slot
            after(e, "V", "flag", s)
            after(e, "P", "aT", s)
            return e.tensor_tensor_scan(Fs[0:H * T, :], flg[u][0:H * T, :], pAT[0:H * T, :], -BIG, ALU.add, ALU.max)

        def v_fm(e, s):
            u = s.slot
            after(e, "P", "Fb", s)
            after(e, "V", "last", s)
            return e.tensor_tensor(fm[:, :, 0:H], pFb[:, 0:H * T].rearrange("p (h j) -> p j h", h=H),
                                   fw[u][:, :, 2 * H:2 * H + 1].to_broadcast([128, T, H]), ALU.mult)

        def v_fhi(e, s):
            after(e, "V", "fm", s)
            return e.tensor_copy(fw[s.slot][:, :, 0:H], fm[:, :, 0:H])

        def v_flo(e, s):
            u = s.slot
            after(e, "V", "fhi", s)
            return e.tensor_tensor(fw[u][:, :, H:2 * H], fm[:, :, 0:H], fw[u][:, :, 0:H], ALU.subtract)

        NM = 2 * H + 1
        pmn = pMn[:, 0:(T + 1) * NM].rearrange("p (j h) -> p j h", h=NM)
        pme = pMe[:, 0:T * NM].rearrange("p (j h) -> p j h", h=NM)

        def v_cr(e, s):
            u = s.slot
            after(e, "V", "cont", s)
            return e.tensor_scalar(cr[:, 0:NM], pme[:, T - 1, :], cont[u][:, 0:1], None, ALU.mult)

        def v_pbm(e, s):
            after(e, "P", f"Mn{T}", s)
            return e.tensor_scalar(pbm[:, :], pmn[:, :, 2 * H], -1.0, BIG, ALU.add, ALU.mult)

        def v_X1(e, s):
            after(e, "V", "pbm", s)
            return e.tensor_tensor(X1[:, 0:H, :], pmn[:, :, 0:H].rearrange("p j h -> p h j"),
                                   pbm[:, :].unsqueeze(1).to_broadcast([W, H, T + 1]), ALU.add)

        def v_X(e, s):
            after(e, "V", "X1", s)
            return e.tensor_tensor(X[:, 0:H, :], pmn[:, :, H:2 * H].rearrange("p j h -> p h j"),
                                   X1[:, 0:H, :], ALU.add)

        def v_Mm(e, s):
            after(e, "V", "X", s)
            return e.tensor_reduce(Mm[:, 0:H], X[:, 0:H, :], AX.X, ALU.max)

        def v_Mhi(e, s):
            after(e, "V", "Mm", s)
            return e.tensor_copy(Mb[:, 0:H], Mm[:, 0:H])

        def v_Mlo(e, s):
            after(e, "V", "Mhi", s)
            return e.tensor_tensor(Mb[:, H:2 * H], Mm[:, 0:H], Mb[:, 0:H], ALU.subtract)

        def v_df(e, s):
            after(e, "A", "fbw", s - 1)
            return e.tensor_tensor(df[:, 0:H], X[:, 0:H, T], Mm[:, 0:H], ALU.subtract)

        def v_d1(e, s):
            u = s.slot
            after(e, "P", f"Me{T - 1}", s)
            return e.tensor_tensor(d1[:, :, 0:H], al[u][:, 0:H * T].rearrange("p (h j) -> p j h", h=H),
                                   pme[:, :, 0:H], ALU.subtract)

        def v_d(e, s):
            after(e, "V", "d1", s)
            return e.tensor_tensor(dd[:, :, 0:H], d1[:, :, 0:H], pme[:, :, H:2 * H], ALU.subtract)

        def v_vals(e, s):
            u = s.slot
            after(e, "A", "w", s)
            after(e, "V", "vj", s)
            return e.tensor_tensor(
                vals[u][:, :, 0:64].rearrange("p j (h c) -> p j h c", h=H),
                vj[u][:, :, :].rearrange("p j (h c) -> p j h c", h=H),
                vals[u][:, :, 64:64 + H].unsqueeze(3).to_broadcast([128, T, H, C]), ALU.mult)

        base_of = {}

        def v_facc(e, s):
            base_of[s.c] = e.value_load(tbl[0:1, 1, bass.ds(s.value(), 1)], min_val=0, max_val=z.idle)
            after(e, "P", "agg7", s)
            after(e, "V", "acc", s - 1)
            c = acc[0:AR, bass.ds(base_of[s.c], 1)]
            return e.tensor_scalar(c, c, pFac[0:AR, :], None, ALU.mult)

        def v_acc(e, s):
            if att:
                after(e, "V", "facc", s)
            else:
                base_of[s.c] = e.value_load(tbl[0:1, 1, bass.ds(s.value(), 1)], min_val=0, max_val=z.idle)
                after(e, "V", "acc", s - 1)
            after(e, "P", "agg7", s)
            c = acc[0:AR, bass.ds(base_of[s.c], W)]
            return e.tensor_tensor(c, c, pG[0:AR, 0:64], ALU.add)

        def p_e0(e, s):
            u = s.slot
            ge16(e, s_l, NL, s)
            if att:
                after(e, "V", "vj", s - 3)
                return e.matmul(pE[u][:, 0:256], ea[u][:, 0:128], bd32[:, l, :], start=True, stop=True)
            after(e, "A", "relu", s - 3)
            return e.matmul(pE[u][:, :], ea[u][:, 0:128], bd16[:, :], start=True, stop=False)

        def p_e1(e, s):
            u = s.slot
            return e.matmul(pE[u][:, 256:512], ea[u][:, 128:256], bd32[:, l, :], start=True, stop=True)

        def p_OT(e, s, m):
            u = s.slot
            if m == 0:
                after(e, "A", "Ob", s)
                hold(e)
            return e.transpose(pOT[:, 128 * m:128 * m + 128], Ob[u][:, m, :], idb[:, :])

        def p_q(e, s, n):
            u = s.slot
            j, k = n // 3, n % 3
            if n == 0:
                after(e, "A", "OTs", s)
                hold(e)
            out = pQ if att else pE[u]
            return e.matmul(out[:, 64 * j:64 * j + 64], OTs[u][:, j, :], qw[u][:, 64 * k:64 * k + 64],
                            start=att and k == 0, stop=k == 2 if att else n == 3 * T - 1)

        def p_aT(e, s):
            u = s.slot
            after(e, "V", "alpha", s)
            hold(e)
            return e.transpose(pAT[0:H * T, :], al[u][:, 0:H * T], ident[:, :])

        def p_Fb(e, s):
            after(e, "V", "scan", s)
            hold(e)
            return e.transpose(pFb[:, 0:H * T], Fs[0:H * T, :], ident[0:H * T, 0:H * T])

        def p_Mn(e, s, j):
            u = s.slot
            if j == 0:
                after(e, "V", "cr", s)
                hold(e)
            lhs = cmb[:, :] if j == T else Ob[u][:, j, :]
            rhs = cr[:, 0:NM] if j == T else fw[u][:, j, 0:NM]
            return e.matmul(pmn[:, j, :], lhs, rhs, start=True, stop=True)

        def p_Me(e, s, j):
            u = s.slot
            if j == 0:
                after(e, "V", "Mlo", s)
                hold(e)
            return e.matmul(pme[:, j, :], OTs[u][:, j, :], Mb[:, 0:NM],
                            start=True, stop=True)

        def p_agg(e, s, j):
            u = s.slot
            if j == 0:
                if att:
                    after(e, "V", "vals", s)
                else:
                    after(e, "A", "relu", s)
                after(e, "V", "acc", s - 1)
            return e.matmul(pG[0:AR, 0:64], vals[u][:, j, 0:AR], O[u][:, j, :], start=j == 0, stop=j == T - 1)

        def p_fac(e, s):
            after(e, "A", "fbw", s)
            after(e, "V", "acc", s - 1)
            return e.matmul(pFac[0:AR, :], fb[:, 0:AR], e0[:, :], start=True, stop=True)

        def a_tb(e, s):
            u = s.slot
            ge16(e, s_l, NL, s)
            after(e, "V", "flag", s - 3)
            return e.activation(tb[u][0:H * T, :], dr[u][0:H * T, :], ACT.Identity, scale=BIG)

        def a_Ob(e, s):
            u = s.slot
            after(e, "V", "O", s)
            after(e, "P", f"Mn{T}" if att else "OT7", s - 3)
            return e.activation(Ob[u][:, :, :], O[u][:, :, :], ACT.Copy)

        def a_OTs(e, s):
            u = s.slot
            after(e, "P", "OT7", s)
            after(e, "P", "Me7" if att else "q23", s - 3)
            return e.activation(OTs[u][:, :, :], pOT[:, :].rearrange("p (a b) -> p a b", a=T), ACT.Copy)

        def a_fb(e, s):
            after(e, "V", "df", s)
            after(e, "P", "fac", s - 1)
            return e.activation(
                fb[:, 0:64].rearrange("p (h c) -> p h c", h=H),
                df[:, 0:H].unsqueeze(2).to_broadcast([W, H, C]), ACT.Exp, scale=scale)

        def a_fbw(e, s):
            return e.activation(fb[:, 64:64 + H], df[:, 0:H], ACT.Exp, scale=scale)

        def a_w(e, s):
            u = s.slot
            after(e, "V", "d", s)
            after(e, "P", "agg7", s - 3)
            return e.activation(vals[u][:, :, 64:64 + H], dd[:, :, 0:H], ACT.Exp, scale=scale)

        def a_relu(e, s):
            u = s.slot
            after(e, "P", "q23", s)
            after(e, "P", "agg7", s - 3)
            return e.activation(vals[u][:, :, 0:64], pE[u][:, :].rearrange("p (j c) -> p j c", c=64), ACT.Relu)

        table = {"V": dict(fm=v_fm, fhi=v_fhi, flo=v_flo, X1=v_X1, Mhi=v_Mhi, Mlo=v_Mlo, d1=v_d1, O=v_O, last=v_last, cont=v_cont, kj=v_kj, vj=v_vj, prod=v_prod, alpha=v_alpha,
                           flag=v_flag, scan=v_scan, cr=v_cr, pbm=v_pbm, X=v_X, Mm=v_Mm, df=v_df,
                           d=v_d, vals=v_vals, facc=v_facc, acc=v_acc),
                 "P": dict(e0=p_e0, e1=p_e1, OT=p_OT, q=p_q, aT=p_aT, Fb=p_Fb, Mn=p_Mn, Me=p_Me, agg=p_agg,
                           fac=p_fac),
                 "A": dict(tb=a_tb, OTs=a_OTs, Ob=a_Ob, fb=a_fb, fbw=a_fbw, w=a_w, relu=a_relu)}

        def emit(e, k, t, stages):
            for n, o in enumerate(order[k]):
                if o[0] not in stages:
                    t4 = t + BIAS
                    e.wait_ge(prog[k], t4.times(3 * K[k], 0) + t4.c % 3 * K[k] + n)
                    e.sem_inc(prog[k], 1)
                    continue
                s = t + lead[o[0]]
                f = table[k].get(o[2:])
                if f is None:
                    part = o[2:].rstrip("0123456789")
                    table[k][part](e, s, int(o[2 + len(part):])).then_inc(prog[k], 1)
                else:
                    f(e, s).then_inc(prog[k], 1)

        def count_of(e):
            return e.value_load(ntr[0:1, 0:1], min_val=1, max_val=(SM - 3 - z.peel) // 3)

        def engine(k):
            def run(e):
                for w in start[k]:
                    e.wait_ge(*w)
                e.sem_inc(prog[k], (BIAS - 2) * K[k])
                n = count_of(e)
                emit(e, k, At(0, -2), "Z")
                emit(e, k, At(0, -1), "ZA")
                emit(e, k, At(0, 0), "ZAB")
                for c in range(1, 1 + z.peel):
                    emit(e, k, At(0, c), "ZABC")
                with e.Fori(0, n) as i:
                    for c in range(1 + z.peel, 4 + z.peel):
                        emit(e, k, At(i, c), "ZABC")
                emit(e, k, At(n, 1 + z.peel), "ABC")
                emit(e, k, At(n, 2 + z.peel), "BC")
                emit(e, k, At(n, 3 + z.peel), "C")
                e.wait_ge(prog[k], val_end(k, n))
                hold(e)
            return run

        def val_end(k, n):
            return n * (3 * K[k]) + (BIAS + 4 + z.peel) * K[k]

        def loads(e, s):
            u = s.slot
            b = e.value_load(tbl[0:1, 0, bass.ds(s.value(), 1)], min_val=0, max_val=B - 1)
            base = e.value_load(tbl[0:1, 1, bass.ds(s.value(), 1)], min_val=0, max_val=z.idle)
            after(e, "V", "cont" if att else "O", s - 2 if att else s - 3)
            e.dma_start(sdn[u][:, :], a["sdn"][bass.ds(b, 1)].rearrange("a p c -> (a p) c")).then_inc(s_i[u], 16)
            after(e, "P", "q23", s - 3)
            e.dma_start(ea[u][:, 0:eat.shape[2]], eat[bass.ds(b, 1)].rearrange("a p c -> (a p) c")).then_inc(s_l[u], 16)
            e.dma_start(qw[u][:, :], qtab[bass.ds(base, W), :]).then_inc(s_l[u], 16)
            if att:
                after(e, "A", "tb", s - 3)
                for h in range(2):
                    e.dma_start(dr[u][T * h:T * h + T, :],
                                a["dr"][bass.ds(b, 1)].rearrange("a p c -> (a p) c")).then_inc(s_l[u], 16)

        def sync(e):
            for w in ready:
                e.wait_ge(*w)
            n = count_of(e)
            for c in range(3 + z.peel):
                loads(e, At(0, c))
            with e.Fori(0, n) as i:
                for c in range(3 + z.peel, 6 + z.peel):
                    loads(e, At(i, c))

        def gathers(e, s):
            u = s.slot
            ge16(e, s_i, 1, s)
            hold(e)
            after(e, "V", "vj", s - 3)
            hold(e)
            for j in range(T):
                e.indirect_dma_start(G[u][:, j, :], None, kvtab,
                                     bass.IndirectOffsetOnAxis(ap=sdn[u][:, j:j + 1], axis=0)).then_inc(s_g[u], 16)

        def pool(e):
            for w in ready:
                e.wait_ge(*w)
            n = count_of(e)
            for c in range(3 + z.peel):
                gathers(e, At(0, c))
            with e.Fori(0, n) as i:
                for c in range(3 + z.peel, 6 + z.peel):
                    gathers(e, At(i, c))

        for k in "VPA":
            queue[k].append(engine(k))
        queue["S"].append(sync)
        if att:
            queue["G"].append(pool)

    evs = norm_rows(x_t)
    ready = tables(evs, 64, w1[:, :], None, PT)
    vt = last("V")
    edge_pass("m", "mean", 0, 1, {"V": [t_t], "P": [w_t, vt], "A": [t_t]}, PT, None, a["ea16"], ready + [t_t])
    evs = fold("mean", 0, 65)
    out = add_rows(evs)
    evs = norm_rows(out[-1])
    for l in range(3):
        ready = tables(evs, 192, wkvq[:, l, :], KV[l], QT[l])
        vt = op("V", lambda e: e.memset(Mb[:, :], 1.0))
        edge_pass(f"a{l}", "att", l, 2 if l < 2 else 1, {"V": [], "P": [vt], "A": [vt]},
                  QT[l], KV[l], a["ea32"], ready + [t_t])
        evs = fold("mid" if l < 2 else "last", l, 66 if l < 2 else 65)
    out = add_rows(evs)
    s_o = sem("s_o")
    full = N // 128
    o1 = dma("S", s_o, 16, lambda e: e.dma_start(
        a["out"][0:128 * full, :].rearrange("(t p) c -> p t c", p=128), XR[:, 0:full, :]), out[-1])
    if N % 128:
        o1 = dma("S", s_o, 32, lambda e: e.dma_start(a["out"][128 * full:N, :], XR[0:N % 128, full, :]))
    queue["S"].append(lambda e: e.wait_ge(*o1))

    block = ctx.enter_context(nc.Block())

    @block.sync
    def _(e):
        for f in queue["S"]:
            f(e)

    @block.gpsimd
    def _(e):
        for f in queue["G"]:
            f(e)

    @block.scalar
    def _(e):
        for f in queue["A"]:
            f(e)

    @block.vector
    def _(e):
        for f in queue["V"]:
            f(e)

    @block.tensor
    def _(e):
        for f in queue["P"]:
            f(e)


def layout(x, src, dst, edge_attr_16, edge_attr_32, z):
    ep = z.blocks * BE
    out = {}
    xp = np.zeros((z.nc, 64), np.float32)
    xp[:z.n] = x
    out["x"] = xp
    s = np.zeros(ep, np.int32)
    s[:z.e] = src
    d = np.full(ep, z.n, np.int32)
    d[:z.e] = dst
    s3 = s.reshape(z.blocks, T, 128)
    d3 = d.reshape(z.blocks, T, 128)
    nx = np.full((z.blocks, T, 128), -1, np.int32)
    nx[:, :, :127] = d3[:, :, 1:]
    out["sdn"] = np.ascontiguousarray(np.concatenate([s3, d3, nx], axis=1).transpose(0, 2, 1))
    out["dr"] = np.ascontiguousarray(d3)
    dfl = d.reshape(z.blocks, BE)
    out["dst_first"] = np.ascontiguousarray(dfl[:, 0]).reshape(1, -1)
    out["dst_last"] = np.ascontiguousarray(dfl[:, -1]).reshape(1, -1)
    e16 = np.zeros((ep, 16), np.float32)
    e16[:z.e] = edge_attr_16
    out["ea16"] = np.ascontiguousarray(e16.reshape(z.blocks, T, 128, 16).transpose(0, 1, 3, 2)).reshape(
        z.blocks, T * 16, 128)
    e32 = np.zeros((ep, 32), np.float32)
    e32[:z.e] = edge_attr_32
    out["ea32"] = np.ascontiguousarray(e32.reshape(z.blocks, 2, 4, 128, 32).transpose(0, 2, 4, 1, 3)).reshape(
        z.blocks, 128, 256)
    return out


def arrays_of(inputs, z):
    out = layout(*(np.asarray(inputs[k]) for k in ("x", "src", "dst", "edge_attr_16", "edge_attr_32")), z)
    for k in ("W1", "b1", "Wres", "bres"):
        out[k] = np.asarray(inputs["L0_gnn_" + k])
    for l in range(3):
        for k in ("Wq", "bq", "Wk", "bk", "Wv", "bv", "We", "Ws", "bs"):
            out[f"{k}{l}"] = np.asarray(inputs[f"L1_gnn_{k}{l}"])
    out["prelu"] = np.asarray(inputs["L1_gnn_prelu_a"]).reshape(1)
    return out


def kernel(**inputs):
    import concourse.bacc as bacc
    from concourse.bass_utils import run_bass_kernel_spmd

    z = Sizes(inputs["x"].shape[0], inputs["src"].shape[0])
    arrays = arrays_of(inputs, z)
    nc = bacc.Bacc("TRN2", target_bir_lowering=False, num_devices=1)
    a = {k: nc.dram_tensor(f"in_{k}", v.shape, mybir.dt.from_np(v.dtype), kind="ExternalInput").ap()
         for k, v in arrays.items()}
    a["out"] = nc.dram_tensor("out_0", (z.n, 64), F32, kind="ExternalOutput").ap()
    gnn_program(nc, z, a)
    r = run_bass_kernel_spmd(nc, [{f"in_{k}": v for k, v in arrays.items()}], core_ids=[0])
    return r.results[0]["out_0"]
```

```python
import numpy as np
from contextlib import ExitStack

import concourse.bass as bass
from concourse import mybir

F32 = mybir.dt.float32
I32 = mybir.dt.int32
BF16 = mybir.dt.bfloat16
ALU = mybir.AluOpType
ACT = mybir.ActivationFunctionType
AX = mybir.AxisListType
BIG = 2.0 ** 99
EPS = 1e-5

T = 8
BE = 128 * T
BIAS = 6
W = 64
SL = 4


class Sizes:
    def __init__(self, n, e):
        self.n = n
        self.e = e
        self.blocks = -(-e // BE)
        self.blocks += self.blocks % 2
        self.tiles = -(-(n + 1 + W) // 128)
        self.nc = self.tiles * 128
        self.idle = n + 1
        self.peel = (self.blocks - 3) % 3
        self.smax = W + self.blocks + -(-(n + 1) // W) + 3 + 3
        assert self.idle + W <= self.nc and self.smax <= 512


class At:

    def __init__(self, i, c):
        self.i, self.c = i, c

    def __add__(self, d):
        return At(self.i, self.c + d)

    def __sub__(self, d):
        return At(self.i, self.c - d)

    @property
    def slot(self):
        return self.c % 3

    def times(self, k, add):
        return self.i * k + (self.c // 3 * k + add)

    def value(self):
        return self.i * 3 + self.c


def gnn_program(nc, z, a):
    ctx = ExitStack()
    with ctx:
        build(nc, z, a, ctx)


def build(nc, z, a, ctx):
    B, NCOL, NT, SM = z.blocks, z.nc, z.tiles, z.smax
    N = z.n

    def sb(name, shape, dt=F32):
        return ctx.enter_context(nc.sbuf_tensor(name, shape, dt))

    def pb(name, shape, dt=F32):
        return ctx.enter_context(nc.psum_tensor(name, shape, dt))

    def sem(name):
        return ctx.enter_context(nc.semaphore(name))

    XR = sb("XR", [128, NT, 64])
    WK = sb("WK", [128, NT, 64])
    hT = sb("hT", [65, NCOL])
    acc = sb("acc", [66, NCOL])
    SQ = sb("SQ", [128, NT, 64])
    st = sb("st", [128, 4, NT])
    w1 = sb("w1", [65, 64])
    wr = sb("wr", [65, 64])
    bd16 = sb("bd16", [128, T * 64])
    wkvq = sb("wkvq", [65, 3, 192])
    bd32 = sb("bd32", [128, 3, 256])
    wskip = sb("wskip", [65, 3, 64])
    pra = sb("pra", [128, 1])
    dn = sb("dn", [128, 2, 4, 2])
    ident = sb("ident", [128, 128])
    cmat = sb("cmat", [128, W])
    cmb = sb("cmb", [128, W], BF16)
    idb = sb("idb", [128, 128], BF16)
    e0 = sb("e0", [64, 1])
    ioi = sb("ioi", [128, SM], I32)
    iof = sb("iof", [128, SM])
    bf = sb("bf", [128, SM])
    tbl = sb("tbl", [128, 2, SM], I32)
    ntr = sb("ntr", [128, 1], I32)
    fl = sb("fl", [1, 2, B], I32)
    flf = sb("flf", [1, 2, B])
    wi = sb("wi", [1, 2, B], I32)
    pe_ = sb("pe_", [1, 4, B + 1])
    pcol = sb("pcol", [128, 2, 2])
    cmp_ = sb("cmp_", [128, 2, SM])
    dlh = sb("dlh", [128, 2, 128])
    ones = sb("ones", [128, 128])
    n3 = sb("n3", [1, 2, SM])
    stg = sb("stg", [128, SL, 4, 192])
    stq = sb("stq", [128, SL, 4, 192], BF16)
    rq = sb("rq", [128, SL, 4, 64])

    G = [sb(f"G{u}", [128, T, 128]) for u in range(3)]
    sdn = [sb(f"sdn{u}", [128, 3 * T], I32) for u in range(3)]
    ea = [sb(f"ea{u}", [128, 256]) for u in range(3)]
    dr = [sb(f"dr{u}", [16, 128], I32) for u in range(3)]
    qw = [sb(f"qw{u}", [128, 128], BF16) for u in range(3)]
    O = [sb(f"O{u}", [128, T, W]) for u in range(3)]
    Ob = [sb(f"Ob{u}", [128, T, 2, W], BF16) for u in range(3)]
    OTs = [sb(f"OTs{u}", [128, T, 128], BF16) for u in range(3)]
    kj = sb("kj", [128, T, 64])
    vj = [sb(f"vj{u}", [128, T, 64]) for u in range(3)]
    vals = [sb(f"vals{u}", [128, T, 66]) for u in range(3)]
    al = [sb(f"al{u}", [128, 2 * T]) for u in range(3)]
    tb = [sb(f"tb{u}", [16, 128]) for u in range(3)]
    flg = [sb(f"flg{u}", [16, 128]) for u in range(3)]
    Fs = sb("Fs", [16, 128])
    fw = [sb(f"fw{u}", [128, T, 8], BF16) for u in range(3)]
    cont = [sb(f"cont{u}", [128, 1]) for u in range(3)]
    cr = sb("cr", [128, 8], BF16)
    fm = sb("fm", [128, T, 2])
    onb = sb("onb", [1, W], BF16)
    cb = sb("cb", [1, 2, 4 * (T + 1)], BF16)
    lm = [sb(f"lm{u}", [128, T]) for u in range(3)]
    X = sb("X", [W, 2, T + 1])
    Mm = sb("Mm", [W, 2])
    Mb = sb("Mb", [W, 8], BF16)
    d1 = sb("d1", [128, T, 2])
    df = sb("df", [W, 2])
    fb = sb("fb", [W, 66])
    dd = sb("dd", [128, T, 2])

    pE = [pb(f"pE{u}", [128, T * 64]) for u in range(3)]
    pOT = pb("pOT", [128, T * 128], BF16)
    pY = pb("pY", [128, 512])
    pQ = pb("pQ", [128, 512])
    pS = pb("pS", [128, 512])
    pG = pb("pG", [128, 512])
    pAT = pS[0:16, 0:128]
    pFb = pS[:, 128:144]
    pMn = pY[0:W, 0:4 * (T + 1)]
    pMe = pS[:, 256:256 + 6 * T]
    pFac = pG[0:66, 64:65]

    def dram(name, shape, dt=F32):
        return nc.dram_tensor(name, shape, dt, kind="Internal").ap()

    PT = dram("PT", [NCOL, 192], BF16)
    KV = [dram(f"KV{l}", [NCOL, 128]) for l in range(3)]
    QT = [dram(f"QT{l}", [NCOL, 192], BF16) for l in range(3)]

    queue = {k: [] for k in "VAPGS"}
    done = {k: sem(f"done_{k}") for k in "VAPG"}
    count = dict.fromkeys("VAPG", 0)

    def op(k, f, *waits):
        count[k] += 1

        def run(e):
            for s, v in waits:
                e.wait_ge(s, v)
            f(e).then_inc(done[k], 1)
        queue[k].append(run)
        return done[k], count[k]

    def dma(k, s, n, f, *waits):
        def run(e):
            for q, v in waits:
                e.wait_ge(q, v)
            f(e).then_inc(s, 16)
        queue[k].append(run)
        return s, n

    def last(k):
        return done[k], count[k]

    s_w = sem("s_w")
    nw = [0]

    def load(out, src, k="S"):
        nw[0] += 16
        dma(k, s_w, nw[0], lambda e, out=out, src=src: e.dma_start(out, src))

    def row(v, m):
        return v.rearrange("(a m) -> a m", a=1) if m else v

    s_x = sem("s_x")
    s_fl = sem("s_fl")
    x_t = dma("S", s_x, 16, lambda e: e.dma_start(XR[:, :, :], a["x"].rearrange("(t p) c -> p t c", p=128)))
    dma("A", s_fl, 16, lambda e: e.dma_start(fl[:, 0, :], a["dst_first"]))
    fl_t = dma("A", s_fl, 32, lambda e: e.dma_start(fl[:, 1, :], a["dst_last"]))

    zb = op("V", lambda e: e.memset(bd16[:, :], 0.0))
    zb2 = op("V", lambda e: e.memset(bd32[:, :, :], 0.0))
    queue["S"].append(lambda e: e.wait_ge(*zb2))
    load(w1[0:64, :], a["W1"][0:64, :])
    load(w1[64:65, :], row(a["b1"], 1))
    load(wr[0:64, :], a["Wres"])
    load(wr[64:65, :], row(a["bres"], 1))
    for j in range(T):
        load(bd16[16 * j:16 * j + 16, 64 * j:64 * j + 64], a["W1"][64:80, :])
    for l in range(3):
        for m, c in enumerate("kvq"):
            load(wkvq[0:64, l, 64 * m:64 * m + 64], a[f"W{c}{l}"])
            load(wkvq[64:65, l, 64 * m:64 * m + 64], row(a[f"b{c}{l}"], 1))
        for j in range(4):
            load(bd32[32 * j:32 * j + 32, l, 64 * j:64 * j + 64], a[f"We{l}"])
        load(wskip[0:64, l, :], a[f"Ws{l}"])
        load(wskip[64:65, l, :], row(a[f"bs{l}"], 1))
    load(pra[:, :], a["prelu"].rearrange("(a m) -> a m", a=1).to_broadcast([128, 1]))
    w_t = (s_w, nw[0])

    op("G", lambda e: e.memset(ident[:, :], 0.0))
    op("G", lambda e: e.memset(cmat[:, :], 0.0))
    op("G", lambda e: e.memset(e0[:, :], 0.0))
    g0 = op("G", lambda e: e.memset(ones[:, :], 1.0))
    op("G", lambda e: e.affine_select(out=ident[:, :], in_=ident[:, :], compare_op=ALU.not_equal, fill=1.0,
                                      base=0, pattern=[[-1, 128]], channel_multiplier=1), g0)
    op("G", lambda e: e.affine_select(out=cmat[:, :], in_=cmat[:, :], compare_op=ALU.not_equal, fill=1.0,
                                      base=-127, pattern=[[128, W]], channel_multiplier=1))
    op("G", lambda e: e.affine_select(out=e0[:, :], in_=e0[:, :], compare_op=ALU.not_equal, fill=1.0,
                                      base=0, pattern=[[1, 1]], channel_multiplier=1))
    op("G", lambda e: e.iota(ioi[:, :], pattern=[[1, SM]], base=0, channel_multiplier=0))
    g_t = last("G")
    one_t = op("G", lambda e: e.memset(hT[64:65, :], 1.0), g_t)
    op("G", lambda e: e.memset(acc[:, :], 0.0), one_t)
    op("V", lambda e: e.tensor_copy(cmb[:, :], cmat[:, :]), g_t)
    op("V", lambda e: e.tensor_copy(idb[:, :], ident[:, :]), g_t)
    io_t = op("V", lambda e: e.tensor_copy(iof[:, :], ioi[:, :]), g_t)

    op("V", lambda e: e.tensor_copy(flf[:, :, :], fl[:, :, :]), fl_t)
    v = op("V", lambda e: e.tensor_tensor(wi[:, 0, :], fl[:, 1, :], fl[:, 0, :], ALU.subtract))
    v = op("V", lambda e: e.tensor_scalar(wi[:, 1, :], wi[:, 0, :], 6, None, ALU.arith_shift_right), v)
    v = op("V", lambda e: e.memset(pe_[:, :, :], 0.0), v)
    v = op("V", lambda e: e.memset(pe_[:, 3, :], 1.0), v)
    v = op("V", lambda e: e.tensor_copy(pe_[:, 0, 0:B], wi[:, 1, :]), v)
    v = op("V", lambda e: e.tensor_scalar(pe_[:, 0, 0:B], pe_[:, 0, 0:B], 1.0, None, ALU.add), v)
    v = op("V", lambda e: e.tensor_tensor_scan(pe_[:, 1, 1:B + 1], pe_[:, 3, 0:B], pe_[:, 0, 0:B], 0.0,
                                               ALU.mult, ALU.add), v)
    v = op("V", lambda e: e.scalar_tensor_tensor(pe_[:, 2, 0:B], pe_[:, 1, 0:B], -float(W), flf[:, 0, :],
                                                 ALU.mult, ALU.add), v)
    v = op("V", lambda e: e.tensor_tensor(pe_[:, 0, 0:B - 1], pe_[:, 2, 1:B], pe_[:, 2, 0:B - 1], ALU.subtract), v)
    v = op("V", lambda e: e.memset(pe_[:, 0, B - 1:B], 0.0), v)
    HB = B // 2
    for k in range(2):
        op("P", lambda e, k=k: e.matmul(pQ[0:HB, k:k + 1], pe_[:, 1, 1 + k:B + 1:2], ones[0:1, 0:1],
                                        start=True, stop=True), v, g_t)
        op("P", lambda e, k=k: e.matmul(pQ[0:HB, 2 + k:3 + k], pe_[:, 0, k:B:2], ones[0:1, 0:1],
                                        start=True, stop=True))
    p = op("P", lambda e: e.matmul(pQ[:, 4:5], ones[0:1, :], flf[:, 0, 0:1], start=True, stop=True))
    v = op("V", lambda e: e.tensor_copy(pcol[0:HB, :, :], pQ[0:HB, 0:4].rearrange("p (a b) -> p a b", a=2)), p)
    f0 = sb("f0", [128, 1])
    op("V", lambda e: e.tensor_copy(f0[:, :], pQ[:, 4:5]))
    for k in range(2):
        op("V", lambda e, k=k: e.tensor_scalar(cmp_[0:HB, k, :], iof[0:HB, :], pcol[0:HB, 0, k:k + 1], None,
                                               ALU.is_ge), v)
        v2 = op("V", lambda e, k=k: e.tensor_scalar(dlh[0:HB, k, :], ones[0:HB, :], pcol[0:HB, 1, k:k + 1], None,
                                                    ALU.mult))
    for k in range(2):
        op("P", lambda e, k=k: e.matmul(pS[:, 0:SM], ones[0:HB, :], cmp_[0:HB, k, :],
                                        start=k == 0, stop=k == 1), v2)
    for k in range(2):
        p = op("P", lambda e, k=k: e.matmul(pG[:, 0:SM], dlh[0:HB, k, :], cmp_[0:HB, k, :],
                                            start=k == 0, stop=k == 1))
    idle = float(z.idle)
    v = op("V", lambda e: e.scalar_tensor_tensor(bf[:, :], iof[:, :], float(W), pG[:, 0:SM], ALU.mult, ALU.add), p)
    v = op("V", lambda e: e.tensor_scalar(bf[:, :], bf[:, :], f0[:, 0:1], idle, ALU.add, ALU.min), v)
    v3 = op("V", lambda e: e.tensor_scalar(cmp_[:, 0, :], pS[:, 0:SM], float(B), idle, ALU.is_ge, ALU.mult), v)
    v = op("V", lambda e: e.tensor_tensor(bf[:, :], bf[:, :], cmp_[:, 0, :], ALU.max), v3)
    op("V", lambda e: e.tensor_copy(tbl[:, 1, :], bf[:, :]), v)
    op("V", lambda e: e.tensor_scalar(tbl[:, 0, :], pS[:, 0:SM], float(B - 1), None, ALU.min))
    v = op("V", lambda e: e.tensor_scalar(n3[:, 0, :], iof[0:1, :], 3.0, 4.0 + z.peel, ALU.mult, ALU.add))
    v = op("V", lambda e: e.tensor_scalar(n3[:, 0, :], n3[:, 0, :], pe_[:, 1, B:B + 1], None, ALU.is_le), v)
    v = op("V", lambda e: e.tensor_reduce(n3[:, 1, 0:1], n3[:, 0, :], AX.X, ALU.add), v)
    t_t = op("V", lambda e: e.tensor_copy(ntr[0:1, :], n3[:, 1, 0:1]), v)
    op("V", lambda e: e.memset(pMe, 0.0))
    op("V", lambda e: e.memset(onb[:, :], 1.0))
    c0 = op("V", lambda e: e.memset(cb[:, :, :], 0.0))
    for h in range(2):
        op("V", lambda e, h=h: e.memset(cb[:, h, 0:(T + 1) * (2 * h + 2)].rearrange(
            "p (j m) -> p j m", m=2 * h + 2)[:, :, 0:h + 1], -BIG), c0)
    for u in range(3):
        op("V", lambda e, u=u: e.memset(flg[u][:, :], 0.0))
        op("V", lambda e, u=u: e.memset(vals[u][:, :, 64:66], 1.0))

    NG = -(-NT // 4)
    tiles_of = [min(4, NT - 4 * c) for c in range(NG)]
    freed = {}

    def use(bank):
        return [freed[bank]] if bank in freed else []

    def norm_rows(c0, c1, ready):
        ts = slice(4 * c0, min(4 * c1, NT))
        nt_ = ts.stop - ts.start

        def wide(k):
            return st[:, k, ts].unsqueeze(2).to_broadcast([128, nt_, 64])

        v = op("V", lambda e: e.tensor_reduce(st[:, 0, ts], XR[:, ts, :], AX.X, ALU.add), ready)
        v = op("V", lambda e: e.tensor_scalar(st[:, 0, ts], st[:, 0, ts], 1.0 / 64, None, ALU.mult), v)
        v = op("V", lambda e: e.tensor_tensor(WK[:, ts, :], XR[:, ts, :], wide(0), ALU.subtract), v)
        v = op("V", lambda e: e.tensor_tensor(SQ[:, ts, :], WK[:, ts, :], WK[:, ts, :], ALU.mult), v)
        v = op("V", lambda e: e.tensor_reduce(st[:, 1, ts], SQ[:, ts, :], AX.X, ALU.add), v)
        v = op("V", lambda e: e.tensor_scalar(st[:, 1, ts], st[:, 1, ts], 1.0 / 64, EPS, ALU.mult, ALU.add), v)
        s = op("A", lambda e: e.activation(st[:, 2, ts], st[:, 1, ts], ACT.Sqrt), v)
        v = op("V", lambda e: e.reciprocal(st[:, 3, ts], st[:, 2, ts]), s)
        return op("V", lambda e: e.tensor_tensor(WK[:, ts, :], WK[:, ts, :], wide(3), ALU.mult), v)

    def to_columns(c, ready, func):
        m = tiles_of[c]
        bank = pE[2]
        for j in range(m):
            pt = op("P", lambda e, j=j: e.transpose(bank[0:64, 128 * j:128 * j + 128], WK[:, 4 * c + j, :],
                                                    ident[:, :]), ready, g_t, *use("E2"))
        freed["E2"] = op("A", lambda e: e.activation(hT[0:64, 512 * c:512 * c + 128 * m],
                                                     bank[0:64, 0:128 * m], func), pt)
        return freed["E2"]

    s_t = [sem(f"s_t{k}") for k in range(SL)]
    nt = [0] * SL

    def table_rows(c, ready, lhs_n, weights, kv, qt):
        g = c % SL
        m4 = tiles_of[c]
        old = [(s_t[g], nt[g])] if nt[g] else []
        for h in range(0, m4, 2):
            m = min(2, m4 - h)
            bank = pE[h // 2]
            for j in range(m):
                pt = op("P", lambda e, h=h, j=j, bank=bank: e.matmul(
                    bank[:, lhs_n * j:lhs_n * j + lhs_n],
                    hT[:, 512 * c + 128 * (h + j):512 * c + 128 * (h + j) + 128],
                    weights, start=True, stop=True), ready, w_t, one_t, *use(h))
            ev = freed[h] = op("A", lambda e, h=h, m=m, bank=bank: e.activation(
                stg[:, g, h:h + m, 0:lhs_n], bank[:, 0:lhs_n * m].rearrange("p (t c) -> p t c", t=m),
                ACT.Copy), pt, *old)
        rows = slice(512 * c, 512 * c + 128 * m4)
        if kv is not None:
            nt[g] += 16
            dma("S", s_t[g], nt[g], lambda e: e.dma_start(
                kv[rows, :].rearrange("(t p) c -> p t c", p=128), stg[:, g, 0:m4, 0:128]), ev)
        src = stg[:, g, 0:m4, lhs_n - 64:lhs_n]
        hi, lo, mi = (stq[:, g, 0:m4, 64 * k:64 * k + 64] for k in range(3))
        rr = rq[:, g, 0:m4, :]
        h_t = op("A", lambda e: e.activation(hi, src, ACT.Copy), ev)
        v = op("V", lambda e: e.tensor_tensor(rr, src, hi, ALU.subtract), h_t)
        v = op("V", lambda e: e.tensor_copy(mi, rr), v)
        v = op("V", lambda e: e.tensor_tensor(lo, rr, mi, ALU.subtract), v)
        nt[g] += 16
        dma("S", s_t[g], nt[g], lambda e: e.dma_start(
            qt[rows, :].rearrange("(t p) c -> p t c", p=128), stq[:, g, 0:m4, :]), v)

    def tables_done():
        return [(s_t[k], nt[k]) for k in range(SL) if nt[k]]

    def fold(c, kind, l, H, ready):
        m = tiles_of[c]
        u = c % 2
        rows = 64 + H
        ra, rb = (pS, pG)[u], (pQ, pY)[u]
        lhs = wr[:, :] if kind == "mean" else wskip[:, l, :]
        for j in range(m):
            cols = slice(512 * c + 128 * j, 512 * c + 128 * j + 128)
            pt = op("P", lambda e, j=j, cols=cols: e.transpose(ra[:, rows * j:rows * j + rows], acc[0:rows, cols],
                                                               ident[0:rows, 0:rows]), ready, *use(f"fold{u}"))
        op("G", lambda e: e.memset(acc[:, 512 * c:512 * c + 128 * m], 0.0), pt)
        for j in range(m):
            cols = slice(512 * c + 128 * j, 512 * c + 128 * j + 128)
            pt = op("P", lambda e, j=j, cols=cols: e.matmul(rb[:, 64 * j:64 * j + 64], hT[:, cols], lhs,
                                                            start=True, stop=True), w_t)
        pr = ra[:, 0:rows * m].rearrange("p (t c) -> p t c", c=rows)
        den = dn[:, u, 0:m, 0:H]
        val = WK[:, 4 * c:4 * c + m, :]
        tmp = SQ[:, 4 * c:4 * c + m, :]
        xr = XR[:, 4 * c:4 * c + m, :]
        skip = rb[:, 0:64 * m].rearrange("p (t c) -> p t c", c=64)
        v = op("V", lambda e: e.tensor_scalar(den, pr[:, :, 64:64 + H], 1.0 if kind == "mean" else 1e-16, None,
                                              ALU.max if kind == "mean" else ALU.add), pt)
        v = op("V", lambda e: e.reciprocal(den, den), v)
        v = op("V", lambda e: e.tensor_tensor(
            tmp.rearrange("p t (h c) -> p t h c", h=H), pr[:, :, 0:64].rearrange("p t (h c) -> p t h c", h=H),
            den.unsqueeze(3).to_broadcast([128, m, H, 64 // H]), ALU.mult), v)
        v = op("V", lambda e: e.tensor_tensor(val, tmp, skip, ALU.add), v)
        freed[f"fold{u}"] = v
        if kind == "mean":
            return op("V", lambda e: e.scalar_tensor_tensor(xr, val, 0.0, xr, ALU.max, ALU.add), v)
        if kind == "last":
            return op("V", lambda e: e.tensor_tensor(xr, xr, val, ALU.add), v)
        v = op("V", lambda e: e.tensor_scalar(tmp, val, 0.0, pra[:, 0:1], ALU.min, ALU.mult), v)
        return op("V", lambda e: e.scalar_tensor_tensor(val, val, 0.0, tmp, ALU.max, ALU.add), v)

    spare = sem("spare")

    def edge_pass(name, kind, l, heads, start, qtab, kvtab, eat, ready):
        H, C = heads, 64 // heads
        scale = 1.0 / float(np.sqrt(np.float32(C)))
        att = kind == "att"
        AR = 64 + H
        if att:
            order = {
                "V": ["B fhi", "B fm", "B flo", "B cr", "A kj", "B X", "B Mhi", "B Mm", "B Mlo",
                      "B df", "A vj", "B d1", "B d", "Z cont", "Z last", "B vals", "A prod", "A alpha",
                      "A flag", "C facc", "C acc", "A scan", "Z O"],
                "P": ["B Fb", "B Mc"] + [f"B Mf{j}" for j in range(T)] + [f"B Mn{j}" for j in range(T)]
                     + [f"B Mf{T}", f"B Mn{T}"] + [f"A OT{m}" for m in range(T)]
                     + [f"B Me{j}" for j in range(T)] + ["C fac"] + [f"C agg{j}" for j in range(4)]
                     + [f"A q{j}" for j in range(2 * T)] + [f"C agg{j}" for j in range(4, T)]
                     + ["Z e0", "A aT", "Z e1"],
                "A": ["A tb", "A OTs", "B w", "B fb", "B fbw", "Z lb", "Z Ob"],
            }
        else:
            order = {
                "V": ["Z O", "C acc"],
                "P": ["A e0"] + [f"B agg{j}" for j in range(T)] + [f"A q{j}" for j in range(2 * T)]
                     + [f"Z OT{m}" for m in range(T)],
                "A": ["Z Ob", "A relu", "Z OTs"],
            }
        lead = {"Z": 2, "A": 1, "B": 0, "C": -1}
        prog = {k: sem(f"{name}_{k}") for k in "VPA"}
        s_i = [sem(f"{name}_i{u}") for u in range(3)]
        s_e = [sem(f"{name}_e{u}") for u in range(3)]
        s_l = [sem(f"{name}_l{u}") for u in range(3)]
        s_g = [sem(f"{name}_g{u}") for u in range(3)]
        stage = {k: {o[2:]: o[0] for o in order[k]} for k in order}
        pos = {k: {o[2:]: n for n, o in enumerate(order[k])} for k in order}
        K = {k: len(order[k]) for k in order}
        NL = 4 if att else 2

        def val(k, o, s):
            t4 = s + (BIAS - lead[stage[k][o]])
            return t4.times(3 * K[k], 0) + (t4.c % 3) * K[k] + pos[k][o] + 1

        def after(e, k, o, s):
            e.wait_ge(prog[k], val(k, o, s))

        def hold(e):
            e.sem_inc(spare, 1)

        def ge16(e, sems, per, s):
            e.wait_ge(sems[s.slot], s.times(16 * per, 16 * per))

        def v_O(e, s):
            u = s.slot
            ge16(e, s_i, 1, s)
            after(e, "P", "agg7", s - 3)
            return e.scalar_tensor_tensor(
                O[u][:, :, :], sdn[u][:, T:2 * T].unsqueeze(2).to_broadcast([128, T, W]),
                bf[:, bass.ds(s.value(), 1)],
                iof[:, 0:W].unsqueeze(1).to_broadcast([128, T, W]), ALU.subtract, ALU.is_equal)

        def v_last(e, s):
            u = s.slot
            ge16(e, s_i, 1, s)
            return e.tensor_tensor(lm[u][:, :], sdn[u][:, T:2 * T], sdn[u][:, 2 * T:3 * T], ALU.not_equal)

        def v_cont(e, s):
            u, before = s.slot, (s - 1).slot
            if isinstance(s.i, int) and s.i == 0 and s.c == 0:
                return e.memset(cont[u][:, :], 0.0)
            ge16(e, s_i, 1, s - 1)
            return e.tensor_scalar(cont[u][:, :], sdn[before][:, 2 * T - 1:2 * T],
                                   bf[:, bass.ds(s.value(), 1)], None, ALU.is_equal)

        def v_kj(e, s):
            u = s.slot
            ge16(e, s_g, T, s)
            after(e, "P", "e1", s)
            after(e, "V", "alpha", s - 1)
            return e.tensor_tensor(kj[:, :, :], G[u][:, :, 0:64],
                                   pE[u][:, :].rearrange("p (j c) -> p j c", c=64), ALU.add)

        def v_vj(e, s):
            u = s.slot
            return e.tensor_tensor(vj[u][:, :, :], G[u][:, :, 64:128],
                                   pE[u][:, :].rearrange("p (j c) -> p j c", c=64), ALU.add)

        def v_prod(e, s):
            after(e, "V", "kj", s)
            after(e, "P", "q15", s)
            return e.tensor_tensor(kj[:, :, :], kj[:, :, :], pQ[:, :].rearrange("p (j c) -> p j c", c=64), ALU.mult)

        def v_alpha(e, s):
            u = s.slot
            after(e, "V", "prod", s)
            return e.tensor_reduce(al[u][:, 0:H * T].rearrange("p (h j) -> p j h", h=H),
                                   kj[:, :, :].rearrange("p j (h c) -> p j h c", h=H), AX.X, ALU.add)

        def v_flag(e, s):
            u = s.slot
            after(e, "A", "tb", s)
            return e.tensor_tensor(flg[u][0:H * T, 1:128], tb[u][0:H * T, 0:127], tb[u][0:H * T, 1:128],
                                   ALU.subtract)

        def v_scan(e, s):
            u = s.slot
            after(e, "V", "flag", s)
            after(e, "P", "aT", s)
            return e.tensor_tensor_scan(Fs[0:H * T, :], flg[u][0:H * T, :], pAT[0:H * T, :], -BIG, ALU.add, ALU.max)

        def masked(e, s, out):
            return e.tensor_tensor(out, pFb[:, 0:H * T].rearrange("p (h j) -> p j h", h=H),
                                   lm[s.slot][:, :].unsqueeze(2).to_broadcast([128, T, H]), ALU.mult)

        def v_fhi(e, s):
            after(e, "P", "Fb", s)
            after(e, "V", "last", s)
            after(e, "P", f"Mn{T}", s - 3)
            return masked(e, s, fw[s.slot][:, :, 0:H])

        def v_fm(e, s):
            return masked(e, s, fm[:, :, 0:H])

        def v_flo(e, s):
            u = s.slot
            after(e, "V", "fm", s)
            return e.tensor_tensor(fw[u][:, :, H:2 * H], fm[:, :, 0:H], fw[u][:, :, 0:H], ALU.subtract)

        pmn = pMn[:, 0:(T + 1) * 2 * H].rearrange("p (j h) -> p j h", h=2 * H)
        pme = pMe[:, 0:T * 3 * H].rearrange("p (j h) -> p j h", h=3 * H)

        def v_cr(e, s):
            u = s.slot
            after(e, "V", "cont", s)
            return e.tensor_scalar(cr[:, 0:3 * H], pme[:, T - 1, :], cont[u][:, 0:1], None, ALU.mult)

        def v_X(e, s):
            after(e, "P", f"Mn{T}", s)
            return e.tensor_reduce(X[:, 0:H, :], pmn.rearrange("p j (k h) -> p h j k", h=H), AX.X, ALU.add)

        def v_Mhi(e, s):
            after(e, "V", "X", s)
            return e.tensor_reduce(Mb[:, 0:H], X[:, 0:H, :], AX.X, ALU.max)

        def v_Mm(e, s):
            return e.tensor_reduce(Mm[:, 0:H], X[:, 0:H, :], AX.X, ALU.max)

        def v_Mlo(e, s):
            after(e, "V", "Mm", s)
            return e.tensor_tensor(Mb[:, H:2 * H], Mm[:, 0:H], Mb[:, 0:H], ALU.subtract)

        def v_df(e, s):
            after(e, "A", "fbw", s - 1)
            return e.tensor_tensor(df[:, 0:H], X[:, 0:H, T], Mm[:, 0:H], ALU.subtract)

        def v_d1(e, s):
            u = s.slot
            after(e, "P", f"Me{T - 1}", s)
            return e.tensor_tensor(d1[:, :, 0:H], al[u][:, 0:H * T].rearrange("p (h j) -> p j h", h=H),
                                   pme[:, :, 0:H], ALU.subtract)

        def v_d(e, s):
            after(e, "V", "d1", s)
            return e.tensor_tensor(dd[:, :, 0:H], d1[:, :, 0:H], pme[:, :, H:2 * H], ALU.subtract)

        def v_vals(e, s):
            u = s.slot
            after(e, "A", "w", s)
            after(e, "V", "vj", s)
            return e.tensor_tensor(
                vals[u][:, :, 0:64].rearrange("p j (h c) -> p j h c", h=H),
                vj[u][:, :, :].rearrange("p j (h c) -> p j h c", h=H),
                vals[u][:, :, 64:64 + H].unsqueeze(3).to_broadcast([128, T, H, C]), ALU.mult)

        base_of = {}

        def v_facc(e, s):
            base_of[s.c] = e.value_load(tbl[0:1, 1, bass.ds(s.value(), 1)], min_val=0, max_val=z.idle)
            after(e, "P", "agg7", s)
            after(e, "V", "acc", s - 1)
            c = acc[0:AR, bass.ds(base_of[s.c], 1)]
            return e.tensor_scalar(c, c, pFac[0:AR, :], None, ALU.mult)

        def v_acc(e, s):
            if att:
                after(e, "V", "facc", s)
            else:
                base_of[s.c] = e.value_load(tbl[0:1, 1, bass.ds(s.value(), 1)], min_val=0, max_val=z.idle)
                after(e, "V", "acc", s - 1)
            after(e, "P", "agg7", s)
            c = acc[0:AR, bass.ds(base_of[s.c], W)]
            return e.tensor_tensor(c, c, pG[0:AR, 0:64], ALU.add)

        def p_e0(e, s):
            u = s.slot
            ge16(e, s_e, 1, s)
            if att:
                after(e, "V", "vj", s - 3)
                return e.matmul(pE[u][:, 0:256], ea[u][:, 0:128], bd32[:, l, :], start=True, stop=True)
            after(e, "A", "relu", s - 3)
            return e.matmul(pE[u][:, :], ea[u][:, 0:128], bd16[:, :], start=True, stop=False)

        def p_e1(e, s):
            u = s.slot
            return e.matmul(pE[u][:, 256:512], ea[u][:, 128:256], bd32[:, l, :], start=True, stop=True)

        def p_OT(e, s, m):
            u = s.slot
            if m == 0:
                after(e, "A", "Ob", s)
                hold(e)
            return e.transpose(pOT[:, 128 * m:128 * m + 128], Ob[u][:, m, :, :].rearrange("p a b -> p (a b)"), idb[:, :])

        def p_q(e, s, n):
            u = s.slot
            j, k = n // 2, n % 2
            if n == 0:
                after(e, "A", "OTs", s)
                ge16(e, s_l, NL, s)
                hold(e)
            out = pQ if att else pE[u]
            rows = W if k else 128
            return e.matmul(out[:, 64 * j:64 * j + 64], OTs[u][0:rows, j, :], qw[u][0:rows, 64 * k:64 * k + 64],
                            start=att and k == 0, stop=k == 1 if att else n == 2 * T - 1)

        def p_aT(e, s):
            u = s.slot
            after(e, "V", "alpha", s)
            hold(e)
            return e.transpose(pAT[0:H * T, :], al[u][:, 0:H * T], ident[:, :])

        def p_Fb(e, s):
            after(e, "V", "scan", s)
            hold(e)
            return e.transpose(pFb[:, 0:H * T], Fs[0:H * T, :], ident[0:H * T, 0:H * T])

        def p_Mc(e, s):
            after(e, "V", "X", s - 1)
            return e.matmul(pMn[:, 0:(T + 1) * 2 * H], onb[0:1, :], cb[0:1, H - 1, 0:(T + 1) * 2 * H],
                            start=True, stop=False)

        def p_Mf(e, s, j):
            u = s.slot
            if j == 0:
                after(e, "A", "Ob", s)
                hold(e)
            lhs = cmb[:, :] if j == T else Ob[u][:, j, 0, :]
            rhs = cr[:, 2 * H:3 * H] if j == T else fw[u][:, j, 2 * H:3 * H]
            return e.matmul(pmn[:, j, 0:H], lhs, rhs, start=False, stop=False)

        def p_Mn(e, s, j):
            u = s.slot
            if j == 0:
                after(e, "V", "cr", s)
                hold(e)
            lhs = cmb[:, :] if j == T else Ob[u][:, j, 0, :]
            rhs = cr[:, 0:2 * H] if j == T else fw[u][:, j, 0:2 * H]
            return e.matmul(pmn[:, j, :], lhs, rhs, start=False, stop=j == T)

        def p_Me(e, s, j):
            u = s.slot
            if j == 0:
                after(e, "V", "Mlo", s)
                hold(e)
            return e.matmul(pme[:, j, :], OTs[u][0:W, j, :], Mb[:, 0:3 * H],
                            start=True, stop=True)

        def p_agg(e, s, j):
            u = s.slot
            if j == 0:
                if att:
                    after(e, "V", "vals", s)
                else:
                    after(e, "A", "relu", s)
                after(e, "V", "acc", s - 1)
            return e.matmul(pG[0:AR, 0:64], vals[u][:, j, 0:AR], O[u][:, j, :], start=j == 0, stop=j == T - 1)

        def p_fac(e, s):
            after(e, "A", "fbw", s)
            after(e, "V", "acc", s - 1)
            return e.matmul(pFac[0:AR, :], fb[:, 0:AR], e0[:, :], start=True, stop=True)

        def a_tb(e, s):
            u = s.slot
            ge16(e, s_l, NL, s)
            after(e, "V", "flag", s - 3)
            return e.activation(tb[u][0:H * T, :], dr[u][0:H * T, :], ACT.Identity, scale=BIG)

        def a_lb(e, s):
            u = s.slot
            after(e, "V", "last", s)
            after(e, "P", f"Mn{T}", s - 3)
            return e.activation(fw[u][:, :, 2 * H:3 * H], lm[u][:, :].unsqueeze(2).to_broadcast([128, T, H]),
                                ACT.Copy, scale=BIG)

        def a_Ob(e, s):
            u = s.slot
            after(e, "V", "O", s)
            after(e, "P", f"Mn{T}" if att else "OT7", s - 3)
            return e.activation(Ob[u][:, :, :, :], O[u][:, :, :].unsqueeze(2).to_broadcast([128, T, 2, W]), ACT.Copy)

        def a_OTs(e, s):
            u = s.slot
            after(e, "P", "OT7", s)
            after(e, "P", "Me7" if att else "q15", s - 3)
            return e.activation(OTs[u][:, :, :], pOT[:, :].rearrange("p (a b) -> p a b", a=T), ACT.Copy)

        def a_fb(e, s):
            after(e, "V", "df", s)
            after(e, "P", "fac", s - 1)
            return e.activation(
                fb[:, 0:64].rearrange("p (h c) -> p h c", h=H),
                df[:, 0:H].unsqueeze(2).to_broadcast([W, H, C]), ACT.Exp, scale=scale)

        def a_fbw(e, s):
            return e.activation(fb[:, 64:64 + H], df[:, 0:H], ACT.Exp, scale=scale)

        def a_w(e, s):
            u = s.slot
            after(e, "V", "d", s)
            after(e, "P", "agg7", s - 3)
            return e.activation(vals[u][:, :, 64:64 + H], dd[:, :, 0:H], ACT.Exp, scale=scale)

        def a_relu(e, s):
            u = s.slot
            after(e, "P", "q15", s)
            after(e, "P", "agg7", s - 3)
            return e.activation(vals[u][:, :, 0:64], pE[u][:, :].rearrange("p (j c) -> p j c", c=64), ACT.Relu)

        table = {"V": dict(fm=v_fm, fhi=v_fhi, flo=v_flo, Mhi=v_Mhi, Mlo=v_Mlo, d1=v_d1, O=v_O, last=v_last,
                           cont=v_cont, kj=v_kj, vj=v_vj, prod=v_prod, alpha=v_alpha, flag=v_flag,
                           scan=v_scan, cr=v_cr, X=v_X, Mm=v_Mm, df=v_df, d=v_d, vals=v_vals,
                           facc=v_facc, acc=v_acc),
                 "P": dict(e0=p_e0, e1=p_e1, OT=p_OT, q=p_q, aT=p_aT, Mc=p_Mc, Mf=p_Mf, Fb=p_Fb, Mn=p_Mn,
                           Me=p_Me, agg=p_agg, fac=p_fac),
                 "A": dict(tb=a_tb, lb=a_lb, OTs=a_OTs, Ob=a_Ob, fb=a_fb, fbw=a_fbw, w=a_w, relu=a_relu)}

        def emit(e, k, t, stages):
            t4 = t + BIAS
            n = 0
            while n < K[k]:
                o = order[k][n]
                if o[0] not in stages:
                    m = n
                    while m < K[k] and order[k][m][0] not in stages:
                        m += 1
                    e.wait_ge(prog[k], t4.times(3 * K[k], 0) + t4.c % 3 * K[k] + n)
                    e.sem_inc(prog[k], m - n)
                    n = m
                    continue
                s = t + lead[o[0]]
                f = table[k].get(o[2:])
                if f is None:
                    part = o[2:].rstrip("0123456789")
                    table[k][part](e, s, int(o[2 + len(part):])).then_inc(prog[k], 1)
                else:
                    f(e, s).then_inc(prog[k], 1)
                n += 1

        def count_of(e):
            return e.value_load(ntr[0:1, 0:1], min_val=1, max_val=(SM - 3 - z.peel) // 3)

        def engine(k):
            def run(e):
                for w in start[k]:
                    e.wait_ge(*w)
                e.sem_inc(prog[k], (BIAS - 2) * K[k])
                n = count_of(e)
                emit(e, k, At(0, -2), "Z")
                emit(e, k, At(0, -1), "ZA")
                emit(e, k, At(0, 0), "ZAB")
                for c in range(1, 1 + z.peel):
                    emit(e, k, At(0, c), "ZABC")
                with e.Fori(0, n) as i:
                    for c in range(1 + z.peel, 4 + z.peel):
                        emit(e, k, At(i, c), "ZABC")
                emit(e, k, At(n, 1 + z.peel), "ABC")
                emit(e, k, At(n, 2 + z.peel), "BC")
                emit(e, k, At(n, 3 + z.peel), "C")
                e.wait_ge(prog[k], val_end(k, n))
                hold(e)
            return run

        def val_end(k, n):
            return n * (3 * K[k]) + (BIAS + 4 + z.peel) * K[k]

        def block_of(e, s):
            return e.value_load(tbl[0:1, 0, bass.ds(s.value(), 1)], min_val=0, max_val=B - 1)

        def load_ids(e, s, b=None):
            u = s.slot
            b = block_of(e, s) if b is None else b
            after(e, "V", "cont" if att else "O", s - 2 if att else s - 3)
            if not att:
                hold(e)
            e.dma_start(sdn[u][:, :], a["sdn"][bass.ds(b, 1)].rearrange("a p c -> (a p) c")).then_inc(s_i[u], 16)

        def load_ea(e, s, b):
            u = s.slot
            after(e, "P", "e1" if att else "e0", s - 3)
            if not att:
                hold(e)
            e.dma_start(ea[u][:, 0:eat.shape[2]], eat[bass.ds(b, 1)].rearrange("a p c -> (a p) c")).then_inc(s_e[u], 16)

        def load_rest(e, s, b):
            u = s.slot
            if att:
                load_ea(e, s, b)
            base = e.value_load(tbl[0:1, 1, bass.ds(s.value(), 1)], min_val=0, max_val=z.idle)
            after(e, "P", "q15", s - 3)
            e.dma_start(qw[u][0:W, :], qtab[bass.ds(base, W), 0:128]).then_inc(s_l[u], 16)
            e.dma_start(qw[u][W:128, 0:64], qtab[bass.ds(base, W), 128:192]).then_inc(s_l[u], 16)
            if att:
                after(e, "A", "tb", s - 3)
                for h in range(2):
                    e.dma_start(dr[u][T * h:T * h + T, :],
                                a["dr"][bass.ds(b, 1)].rearrange("a p c -> (a p) c")).then_inc(s_l[u], 16)

        def every(e, f, do):
            for w in start["S"]:
                e.wait_ge(*w)
            n = count_of(e)
            first = [block_of(e, At(0, c)) for c in range(3)]
            for c in range(3):
                f(e, At(0, c), first[c])
            for w in ready:
                e.wait_ge(*w)
            for c in range(3):
                do(At(0, c), first[c], False)
            for c in range(3, 3 + z.peel):
                do(At(0, c), block_of(e, At(0, c)), True)
            with e.Fori(0, n) as i:
                for c in range(3 + z.peel, 6 + z.peel):
                    do(At(i, c), block_of(e, At(i, c)), True)

        def sync(e):
            def do(s, b, ids):
                if ids and att:
                    load_ids(e, s, b)
                load_rest(e, s, b)
            every(e, load_ids if att else lambda *x: None, do)

        def pool_ids(e):
            def do(s, b, ids):
                if ids:
                    load_ids(e, s, b)
                load_ea(e, s, b)
            every(e, load_ids, do)

        def gathers(e, s):
            u = s.slot
            ge16(e, s_i, 1, s)
            hold(e)
            after(e, "V", "vj", s - 3)
            hold(e)
            for j in range(T):
                e.indirect_dma_start(G[u][:, j, :], None, kvtab,
                                     bass.IndirectOffsetOnAxis(ap=sdn[u][:, j:j + 1], axis=0)).then_inc(s_g[u], 16)

        def pool(e):
            for w in ready:
                e.wait_ge(*w)
            n = count_of(e)
            for c in range(3 + z.peel):
                gathers(e, At(0, c))
            with e.Fori(0, n) as i:
                for c in range(3 + z.peel, 6 + z.peel):
                    gathers(e, At(i, c))

        for k in "VPA":
            queue[k].append(engine(k))
        queue["S"].append(sync)
        queue["G"].append(pool if att else pool_ids)

    PART = 4
    parts = [(c, min(c + PART, NG)) for c in range(0, NG, PART)]

    def normed_tables(ready, *to):
        rows = {}
        for n in range(len(parts) + 1):
            before = range(*parts[n - 1]) if n else ()
            if n < len(parts):
                t = ready(*parts[n])
            cols = [to_columns(c, rows[n - 1], ACT.Relu) for c in before]
            if n < len(parts):
                rows[n] = norm_rows(*parts[n], t)
            for c, t in zip(before, cols):
                table_rows(c, t, *to)

    normed_tables(lambda c0, c1: x_t, 64, w1[:, :], None, PT)
    ready = tables_done()
    vt = last("V")
    edge_pass("m", "mean", 0, 1, {"V": [last("G")], "P": [w_t, vt], "A": [t_t],
                                    "S": [t_t]}, PT, None, a["ea16"],
              ready + [t_t])
    vt = prev = op("V", lambda e: e.memset(df[:, :], 0.0))
    normed_tables(lambda c0, c1: [fold(c, "mean", 0, 1, vt) for c in range(c0, c1)][-1],
                  192, wkvq[:, 0, :], KV[0], QT[0])
    for l in range(3):
        ready = tables_done()
        H = 2 if l < 2 else 1
        vt = op("V", lambda e: e.memset(Mb[:, :], BIG))
        edge_pass(f"a{l}", "att", l, H, {"V": [last("G")], "P": [vt], "A": [vt],
                                           "S": [prev]},
                  QT[l], KV[l], a["ea32"], ready + [t_t])
        vt = prev = op("V", lambda e: e.memset(df[:, :], 0.0))
        if l < 2:
            rows, cols = {}, {}
            for c in range(NG + 2):
                if c < NG:
                    rows[c] = fold(c, "mid", l, H, vt)
                if c >= 2:
                    table_rows(c - 2, cols[c - 2], 192, wkvq[:, l + 1, :], KV[l + 1], QT[l + 1])
                if 1 <= c <= NG:
                    cols[c - 1] = to_columns(c - 1, rows[c - 1], ACT.Copy)
    s_o = sem("s_o")
    full = N // 128
    no = 0
    for c0, c1 in parts:
        v = [fold(c, "last", 2, 1, vt) for c in range(c0, c1)][-1]
        t0, t1 = 4 * c0, min(4 * c1, full)
        if t1 > t0:
            no += 16
            dma("S", s_o, no, lambda e, t0=t0, t1=t1: e.dma_start(
                a["out"][128 * t0:128 * t1, :].rearrange("(t p) c -> p t c", p=128), XR[:, t0:t1, :]), v)
    if N % 128:
        no += 16
        dma("S", s_o, no, lambda e: e.dma_start(a["out"][128 * full:N, :], XR[0:N % 128, full, :]), v)
    queue["S"].append(lambda e: e.wait_ge(s_o, no))

    block = ctx.enter_context(nc.Block())

    @block.sync
    def _(e):
        for f in queue["S"]:
            f(e)

    @block.gpsimd
    def _(e):
        for f in queue["G"]:
            f(e)

    @block.scalar
    def _(e):
        for f in queue["A"]:
            f(e)

    @block.vector
    def _(e):
        for f in queue["V"]:
            f(e)

    @block.tensor
    def _(e):
        for f in queue["P"]:
            f(e)


def layout(x, src, dst, edge_attr_16, edge_attr_32, z):
    ep = z.blocks * BE
    out = {}
    xp = np.zeros((z.nc, 64), np.float32)
    xp[:z.n] = x
    out["x"] = xp
    s = np.zeros(ep, np.int32)
    s[:z.e] = src
    d = np.full(ep, z.n, np.int32)
    d[:z.e] = dst
    s3 = s.reshape(z.blocks, T, 128)
    d3 = d.reshape(z.blocks, T, 128)
    nx = np.full((z.blocks, T, 128), -1, np.int32)
    nx[:, :, :127] = d3[:, :, 1:]
    out["sdn"] = np.ascontiguousarray(np.concatenate([s3, d3, nx], axis=1).transpose(0, 2, 1))
    out["dr"] = np.ascontiguousarray(d3)
    dfl = d.reshape(z.blocks, BE)
    out["dst_first"] = np.ascontiguousarray(dfl[:, 0]).reshape(1, -1)
    out["dst_last"] = np.ascontiguousarray(dfl[:, -1]).reshape(1, -1)
    e16 = np.zeros((ep, 16), np.float32)
    e16[:z.e] = edge_attr_16
    out["ea16"] = np.ascontiguousarray(e16.reshape(z.blocks, T, 128, 16).transpose(0, 1, 3, 2)).reshape(
        z.blocks, T * 16, 128)
    e32 = np.zeros((ep, 32), np.float32)
    e32[:z.e] = edge_attr_32
    out["ea32"] = np.ascontiguousarray(e32.reshape(z.blocks, 2, 4, 128, 32).transpose(0, 2, 4, 1, 3)).reshape(
        z.blocks, 128, 256)
    return out


def arrays_of(inputs, z):
    out = layout(*(np.asarray(inputs[k]) for k in ("x", "src", "dst", "edge_attr_16", "edge_attr_32")), z)
    for k in ("W1", "b1", "Wres", "bres"):
        out[k] = np.asarray(inputs["L0_gnn_" + k])
    for l in range(3):
        for k in ("Wq", "bq", "Wk", "bk", "Wv", "bv", "We", "Ws", "bs"):
            out[f"{k}{l}"] = np.asarray(inputs[f"L1_gnn_{k}{l}"])
    out["prelu"] = np.asarray(inputs["L1_gnn_prelu_a"]).reshape(1)
    return out


def kernel(**inputs):
    import concourse.bacc as bacc
    from concourse.bass_utils import run_bass_kernel_spmd

    z = Sizes(inputs["x"].shape[0], inputs["src"].shape[0])
    arrays = arrays_of(inputs, z)
    nc = bacc.Bacc("TRN2", target_bir_lowering=False, num_devices=1)
    a = {k: nc.dram_tensor(f"in_{k}", v.shape, mybir.dt.from_np(v.dtype), kind="ExternalInput").ap()
         for k, v in arrays.items()}
    a["out"] = nc.dram_tensor("out_0", (z.n, 64), F32, kind="ExternalOutput").ap()
    gnn_program(nc, z, a)
    r = run_bass_kernel_spmd(nc, [{f"in_{k}": v for k, v in arrays.items()}], core_ids=[0])
    return r.results[0]["out_0"]
```
